# Optimizing a Trainium2 kernel written in Bass

```python
import numpy as np
import jax
import jax.numpy as jnp

def _softmax(x, axis=-1):
    return jax.nn.softmax(x, axis=axis)

def _gelu(x):
    return jax.nn.gelu(x, approximate=True)

def _silu(x):
    return jax.nn.silu(x)

def _sigmoid(x):
    return jax.nn.sigmoid(x)

def _layernorm(x, axis=-1, eps=1e-05):
    m = jnp.mean(x, axis=axis, keepdims=True)
    v = jnp.var(x, axis=axis, keepdims=True)
    return (x - m) / jnp.sqrt(v + eps)

def _scatter_add(tgt, idx, src, axis=0):
    return tgt.at[idx].add(src)

def _segment_sum(src, seg, n):
    return jax.ops.segment_sum(src, seg, n)
kernel_name = 'mk_decoder_postln_d1_seqx_r8_3f331e'

def setup_inputs(seed: int=0):
    np.random.seed(seed)
    _w = jnp.asarray

    def _rec_inputs():
        import jax
        import jax.numpy as jnp
        _rk = jax.random.key(seed)
        x = 7.22e-05 + 1 * jax.random.normal(jax.random.fold_in(_rk, 1), (4, 512, 128), jnp.float32)
        _lenS = 512 - jax.random.randint(jax.random.fold_in(_rk, 7), (4,), 0, max(1, 512 // 4) + 1, jnp.int32)
        _lenS2 = 77 - jax.random.randint(jax.random.fold_in(_rk, 8), (4,), 0, max(1, 77 // 4) + 1, jnp.int32)
        _ctx_768P = jax.random.normal(jax.random.fold_in(_rk, 11), (4, 16, 96), jnp.float32)
        _ctx_768c = jax.random.dirichlet(jax.random.fold_in(_rk, 511), 0.3 * jnp.ones((16,), jnp.float32), (4, 77))
        _ctx_768t = jnp.einsum('bsk,bkd->bsd', _ctx_768c, _ctx_768P)
        _ctx_768t = _ctx_768t * jax.lax.rsqrt(jnp.mean(jnp.square(_ctx_768t)) + 1e-12) * 0.953939
        ctx_768 = -0.000191848 + 0.999787 * (_ctx_768t + 0.3 * jax.random.normal(jax.random.fold_in(_rk, 611), (4, 77, 96), jnp.float32))
        return (x, ctx_768)
    x, ctx_768 = _rec_inputs()

    def _L0_attn_setup():
        import jax, jax.numpy as jnp
        import numpy as np
        D = 128
        H = 128
        TW = 4
        C_GATE = 8.0

        def _reference_tuple_inner(input_bxtxd, w_x, b_x, w_y, b_y, conv_w, conv_b, gi_w, gi_b, ga_w, ga_b, a_param):
            x = input_bxtxd
            B, T, _ = x.shape
            x1 = jnp.einsum('btd,dh->bth', x, w_x) + b_x
            xp = jnp.pad(x1, ((0, 0), (TW - 1, 0), (0, 0)))
            x2 = sum((conv_w[i] * xp[:, i:i + T, :] for i in range(TW))) + conv_b
            gate_x = jax.nn.sigmoid(jnp.einsum('bth,hk->btk', x2, gi_w) + gi_b)
            gate_a = jax.nn.sigmoid(jnp.einsum('bth,hk->btk', x2, ga_w) + ga_b)
            log_a = -C_GATE * gate_a * jax.nn.softplus(a_param)
            a = jnp.exp(log_a)
            multiplier = jnp.sqrt(jnp.maximum(1.0 - jnp.exp(2.0 * log_a), 0.0))
            multiplier = multiplier.at[:, 0, :].set(1.0)
            a = a.at[:, 0, :].set(0.0)
            normalized_x = gate_x * x2 * multiplier

            def combine(c1, c2):
                a1, h1 = c1
                a2, h2 = c2
                return (a1 * a2, h2 + a2 * h1)
            _, h = jax.lax.associative_scan(combine, (a, normalized_x), axis=1)
            y = jax.nn.gelu(jnp.einsum('btd,dh->bth', x, w_y) + b_y, approximate=False)
            out = h * y
            hn = h[:, -1, :]
            return (out, h, hn)
        key = jax.random.key(seed)
        ks = jax.random.split(key, 12)
        B, T = (8, 512)
        sd = 1.0 / np.sqrt(D)
        sh = 1.0 / np.sqrt(H)
        return {'input_bxtxd': jax.random.normal(ks[0], (B, T, D), jnp.float32), 'w_x': jax.random.normal(ks[1], (D, H), jnp.float32) * sd, 'b_x': jnp.zeros((H,), jnp.float32), 'w_y': jax.random.normal(ks[2], (D, H), jnp.float32) * sd, 'b_y': jnp.zeros((H,), jnp.float32), 'conv_w': jax.random.normal(ks[3], (TW, H), jnp.float32) * 0.5, 'conv_b': jnp.zeros((H,), jnp.float32), 'gi_w': jax.random.normal(ks[4], (H, H), jnp.float32) * sh, 'gi_b': jnp.zeros((H,), jnp.float32), 'ga_w': jax.random.normal(ks[5], (H, H), jnp.float32) * sh, 'ga_b': jnp.zeros((H,), jnp.float32), 'a_param': jax.random.uniform(ks[6], (H,), jnp.float32, 2.0, 6.0)}
    _L0_attn_all = _L0_attn_setup()
    _L0_attn_in = {k: v for k, v in _L0_attn_all.items() if k in ('w_x', 'b_x', 'w_y', 'b_y', 'conv_w', 'conv_b', 'gi_w', 'gi_b', 'ga_w', 'ga_b', 'a_param')}
    del _L0_attn_all

    def _L0_xattn_setup():
        import jax, jax.numpy as jnp
        import numpy as np
        NUM_HEADS = 16
        CLAMP = 10000.0
        key = jax.random.key(seed)
        ks = jax.random.split(key, 8)
        B, Nq, Nkv, Cq, Ckv = (4, 256, 256, 128, 96)
        s_q = 1.0 / np.sqrt(Cq)
        s_kv = 1.0 / np.sqrt(Ckv)
        return {'query': jax.random.normal(ks[0], (B, Nq, Cq), jnp.float32), 'key_value': jax.random.normal(ks[1], (B, Nkv, Ckv), jnp.float32), 'Wq': jax.random.normal(ks[2], (Cq, Cq), jnp.float32) * s_q, 'bq': jnp.zeros((Cq,), jnp.float32), 'Wk': jax.random.normal(ks[3], (Ckv, Cq), jnp.float32) * s_kv, 'bk': jnp.zeros((Cq,), jnp.float32), 'Wv': jax.random.normal(ks[4], (Ckv, Cq), jnp.float32) * s_kv, 'bv': jnp.zeros((Cq,), jnp.float32), 'Wo': jax.random.normal(ks[5], (Cq, Cq), jnp.float32) * s_q, 'bo': jnp.zeros((Cq,), jnp.float32)}
    _L0_xattn_all = _L0_xattn_setup()
    _L0_xattn_in = {k: v for k, v in _L0_xattn_all.items() if k in ('Wq', 'bq', 'Wk', 'bk', 'Wv', 'bv', 'Wo', 'bo')}
    del _L0_xattn_all

    def _L0_ffn_setup():
        import jax, jax.numpy as jnp
        import numpy as np
        TOP_K = 32
        TEMPERATURE = 1.0
        PARAM_SCALE = 0.02

        def _compose_weight(logits, A, B):
            vals, idx = jax.lax.top_k(logits, TOP_K)
            w = jax.nn.softmax(vals / TEMPERATURE)
            A_sel = A[idx]
            B_sel = B[idx]
            return jnp.einsum('k,kir,kro->io', w, A_sel, B_sel)
        key = jax.random.key(seed)
        ks = jax.random.split(key, 7)
        B, S, D, F, P, R = (2, 128, 128, 512, 32, 64)
        x = jax.random.normal(ks[0], (B, S, D), dtype=jnp.float32)
        fc1_A = jax.random.normal(ks[1], (P, D, R), dtype=jnp.float32) * PARAM_SCALE
        fc1_B = jax.random.normal(ks[2], (P, R, F), dtype=jnp.float32) * PARAM_SCALE
        fc2_A = jax.random.normal(ks[3], (P, F, R), dtype=jnp.float32) * PARAM_SCALE
        fc2_B = jax.random.normal(ks[4], (P, R, D), dtype=jnp.float32) * PARAM_SCALE
        fc1_logits = jax.random.normal(ks[5], (P,), dtype=jnp.float32)
        fc2_logits = jax.random.normal(ks[6], (P,), dtype=jnp.float32)
        return {'x': x, 'fc1_A': fc1_A, 'fc1_B': fc1_B, 'fc2_A': fc2_A, 'fc2_B': fc2_B, 'fc1_logits': fc1_logits, 'fc2_logits': fc2_logits}
    _L0_ffn_all = _L0_ffn_setup()
    _L0_ffn_in = {k: v for k, v in _L0_ffn_all.items() if k in ('fc1_A', 'fc1_B', 'fc2_A', 'fc2_B', 'fc1_logits', 'fc2_logits')}
    del _L0_ffn_all
    return {'x': x, 'ctx_768': ctx_768, 'L0_attn_w_x': _L0_attn_in['w_x'], 'L0_attn_b_x': _L0_attn_in['b_x'], 'L0_attn_w_y': _L0_attn_in['w_y'], 'L0_attn_b_y': _L0_attn_in['b_y'], 'L0_attn_conv_w': _L0_attn_in['conv_w'], 'L0_attn_conv_b': _L0_attn_in['conv_b'], 'L0_attn_gi_w': _L0_attn_in['gi_w'], 'L0_attn_gi_b': _L0_attn_in['gi_b'], 'L0_attn_ga_w': _L0_attn_in['ga_w'], 'L0_attn_ga_b': _L0_attn_in['ga_b'], 'L0_attn_a_param': _L0_attn_in['a_param'], 'L0_xattn_Wq': _L0_xattn_in['Wq'], 'L0_xattn_bq': _L0_xattn_in['bq'], 'L0_xattn_Wk': _L0_xattn_in['Wk'], 'L0_xattn_bk': _L0_xattn_in['bk'], 'L0_xattn_Wv': _L0_xattn_in['Wv'], 'L0_xattn_bv': _L0_xattn_in['bv'], 'L0_xattn_Wo': _L0_xattn_in['Wo'], 'L0_xattn_bo': _L0_xattn_in['bo'], 'L0_ffn_fc1_A': _L0_ffn_in['fc1_A'], 'L0_ffn_fc1_B': _L0_ffn_in['fc1_B'], 'L0_ffn_fc2_A': _L0_ffn_in['fc2_A'], 'L0_ffn_fc2_B': _L0_ffn_in['fc2_B'], 'L0_ffn_fc1_logits': _L0_ffn_in['fc1_logits'], 'L0_ffn_fc2_logits': _L0_ffn_in['fc2_logits']}

def reference(x, ctx_768, L0_attn_w_x, L0_attn_b_x, L0_attn_w_y, L0_attn_b_y, L0_attn_conv_w, L0_attn_conv_b, L0_attn_gi_w, L0_attn_gi_b, L0_attn_ga_w, L0_attn_ga_b, L0_attn_a_param, L0_xattn_Wq, L0_xattn_bq, L0_xattn_Wk, L0_xattn_bk, L0_xattn_Wv, L0_xattn_bv, L0_xattn_Wo, L0_xattn_bo, L0_ffn_fc1_A, L0_ffn_fc1_B, L0_ffn_fc2_A, L0_ffn_fc2_B, L0_ffn_fc1_logits, L0_ffn_fc2_logits):
    import jax
    import jax.numpy as jnp

    def _L0_attn_ref(input_bxtxd, w_x, b_x, w_y, b_y, conv_w, conv_b, gi_w, gi_b, ga_w, ga_b, a_param):
        import jax, jax.numpy as jnp
        import numpy as np
        D = 128
        H = 128
        TW = 4
        C_GATE = 8.0

        def _reference_tuple_inner(input_bxtxd, w_x, b_x, w_y, b_y, conv_w, conv_b, gi_w, gi_b, ga_w, ga_b, a_param):
            x = input_bxtxd
            B, T, _ = x.shape
            x1 = jnp.einsum('btd,dh->bth', x, w_x) + b_x
            xp = jnp.pad(x1, ((0, 0), (TW - 1, 0), (0, 0)))
            x2 = sum((conv_w[i] * xp[:, i:i + T, :] for i in range(TW))) + conv_b
            gate_x = jax.nn.sigmoid(jnp.einsum('bth,hk->btk', x2, gi_w) + gi_b)
            gate_a = jax.nn.sigmoid(jnp.einsum('bth,hk->btk', x2, ga_w) + ga_b)
            log_a = -C_GATE * gate_a * jax.nn.softplus(a_param)
            a = jnp.exp(log_a)
            multiplier = jnp.sqrt(jnp.maximum(1.0 - jnp.exp(2.0 * log_a), 0.0))
            multiplier = multiplier.at[:, 0, :].set(1.0)
            a = a.at[:, 0, :].set(0.0)
            normalized_x = gate_x * x2 * multiplier

            def combine(c1, c2):
                a1, h1 = c1
                a2, h2 = c2
                return (a1 * a2, h2 + a2 * h1)
            _, h = jax.lax.associative_scan(combine, (a, normalized_x), axis=1)
            y = jax.nn.gelu(jnp.einsum('btd,dh->bth', x, w_y) + b_y, approximate=False)
            out = h * y
            hn = h[:, -1, :]
            return (out, h, hn)
        return _reference_tuple_inner(input_bxtxd, w_x, b_x, w_y, b_y, conv_w, conv_b, gi_w, gi_b, ga_w, ga_b, a_param)[0]

    def _L0_xattn_ref(query, key_value, Wq, bq, Wk, bk, Wv, bv, Wo, bo):
        import jax, jax.numpy as jnp
        import numpy as np
        NUM_HEADS = 16
        CLAMP = 10000.0
        B, Nq, Cq = query.shape
        Nkv = key_value.shape[1]
        H = NUM_HEADS
        D = Cq // H
        scale = D ** (-0.5)
        q = (query @ Wq + bq).reshape(B, Nq, H, D).transpose(0, 2, 1, 3)
        k = (key_value @ Wk + bk).reshape(B, Nkv, H, D).transpose(0, 2, 1, 3)
        v = (key_value @ Wv + bv).reshape(B, Nkv, H, D).transpose(0, 2, 1, 3)
        attn = jnp.einsum('bhqd,bhkd->bhqk', q, k) * scale
        attn = jnp.clip(attn, -CLAMP, CLAMP)
        attn = jax.nn.softmax(attn, axis=-1)
        attn = jnp.where(jnp.any(jnp.isnan(attn)), jnp.asarray(1.0 / Nkv, attn.dtype), attn)
        x = jnp.einsum('bhqk,bhkd->bqhd', attn, v).reshape(B, Nq, Cq)
        return x @ Wo + bo

    def _L0_ffn_ref(x, fc1_A, fc1_B, fc2_A, fc2_B, fc1_logits, fc2_logits):
        import jax, jax.numpy as jnp
        import numpy as np
        TOP_K = 32
        TEMPERATURE = 1.0
        PARAM_SCALE = 0.02

        def _compose_weight(logits, A, B):
            vals, idx = jax.lax.top_k(logits, TOP_K)
            w = jax.nn.softmax(vals / TEMPERATURE)
            A_sel = A[idx]
            B_sel = B[idx]
            return jnp.einsum('k,kir,kro->io', w, A_sel, B_sel)
        W1 = _compose_weight(fc1_logits, fc1_A, fc1_B)
        W2 = _compose_weight(fc2_logits, fc2_A, fc2_B)
        h = jax.nn.gelu(jnp.einsum('bsd,df->bsf', x, W1))
        return jnp.einsum('bsf,fd->bsd', h, W2)
    x = _layernorm(x + _L0_attn_ref(x, L0_attn_w_x, L0_attn_b_x, L0_attn_w_y, L0_attn_b_y, L0_attn_conv_w, L0_attn_conv_b, L0_attn_gi_w, L0_attn_gi_b, L0_attn_ga_w, L0_attn_ga_b, L0_attn_a_param), axis=-1)
    x = _layernorm(x + _L0_xattn_ref(x, ctx_768, L0_xattn_Wq, L0_xattn_bq, L0_xattn_Wk, L0_xattn_bk, L0_xattn_Wv, L0_xattn_bv, L0_xattn_Wo, L0_xattn_bo), axis=-1)
    x = _layernorm(x + _L0_ffn_ref(x, L0_ffn_fc1_A, L0_ffn_fc1_B, L0_ffn_fc2_A, L0_ffn_fc2_B, L0_ffn_fc1_logits, L0_ffn_fc2_logits), axis=-1)
    return x

_drawn_inputs = setup_inputs


def setup_inputs(seed=0):
    import zlib

    import numpy as np

    out = dict(_drawn_inputs(seed))
    spreads = {'L0_attn_b_x': (0.0, 0.276),
     'L0_attn_b_y': (0.0, 0.285),
     'L0_attn_conv_b': (0.0, 0.1),
     'L0_attn_gi_b': (0.0, 0.79),
     'L0_attn_ga_b': (0.0, 0.8),
     'L0_xattn_bq': (0.0, 0.356),
     'L0_xattn_bk': (0.0, 0.8),
     'L0_xattn_bv': (0.0, 0.1),
     'L0_xattn_bo': (0.0, 0.1)}
    factors = {'L0_attn_ga_w': 8.0,
     'L0_attn_a_param': 8.0,
     'L0_ffn_fc1_A': 8.0,
     'L0_ffn_fc1_B': 8.0,
     'L0_ffn_fc2_A': 8.0,
     'L0_ffn_fc2_B': 8.0,
     'L0_ffn_fc1_logits': 8.0,
     'L0_ffn_fc2_logits': 8.0}
    for name, (base, spread) in spreads.items():
        noise = np.random.default_rng([zlib.crc32(name.encode()), seed]).standard_normal(out[name].shape)
        drawn = base * np.exp(spread * noise) if base else spread * noise
        out[name] = jnp.asarray(drawn.astype(out[name].dtype))
    for name, factor in factors.items():
        out[name] = (out[name] * factor).astype(out[name].dtype)
    return out
```

```python
from contextlib import ExitStack

import numpy as np

import concourse.bass as bass
from concourse import mybir

ALU = mybir.AluOpType
ACT = mybir.ActivationFunctionType
F32 = mybir.dt.float32
AX_X = mybir.AxisListType.X

P = 128
B, T, D = 4, 512, 128
TPB = T // P
NT = B * TPB
M, DC = 77, 96
H = 16
HD = D // H
HH = H // 2
HALF = HH * M
QUAD = 4 * M
RT = -(-HALF // P)
PADW = RT * P
VC = HD + 1
NP_, R, F = 32, 64, 512
KT = NP_ * R // P
FT = F // P
TW = 4
C_GATE = 8.0
CLAMP = 10000.0
SCALE = float(HD) ** -0.5
EPS = 1e-5

V_CW, V_BX, V_BY, V_CB, V_GIB, V_GAB, V_AP, V_BQ, V_N = 0, 4, 5, 6, 7, 8, 9, 10, 11
W_X, W_Y, W_GI, W_GA, W_Q, W_O = range(6)


def build(nc, xT, vecs, wpack, kvpack, bo, logits, a1T, b1, a2T, b2, ident, hmask, vmask, out):
    with ExitStack() as ctx:
        def sb(name, shape, dt=F32):
            return ctx.enter_context(nc.sbuf_tensor(name, shape, dt))

        def sem(name):
            return ctx.enter_context(nc.semaphore(name))

        xc = sb("xc", [P, B, T])
        x1p = sb("x1p", [P, B, T + TW - 1])
        x2 = sb("x2", [P, B, T])
        gx = sb("gx", [P, B, T])
        aa = sb("aa", [P, B, T])
        uu = sb("uu", [P, B, T])
        yy = sb("yy", [P, B, T])
        qT = gx
        x1n = x1p[:].rearrange("p b t -> p (b t)")[:, 0:NT * D].rearrange("p (n d) -> p n d", d=D)
        x2n = aa[:].rearrange("p b (t d) -> p (b t) d", d=D)
        vec = sb("vec", [P, V_N])
        w = sb("w", [P, 6, D])
        kvp = sb("kvp", [DC + 1, B * 3 * M + 2 * D])
        bo_row = sb("bo_row", [1, D])
        ones_row = sb("ones_row", [1, P])
        idn = sb("idn", [P, P])
        hm = sb("hm", [P, H])
        vm = sb("vm", [P, RT, HH])
        lg = sb("lg", [P, 2, NP_])
        lgm = sb("lgm", [P, 2])
        lgs = sb("lgs", [P, 2])
        wsel = sb("wsel", [P, 2, KT])
        spt = sb("spt", [P, 8])
        a1 = sb("a1", [P, KT, D])
        b1s = sb("b1s", [P, KT, F])
        a2 = sb("a2", [P, KT, F])
        b2s = sb("b2s", [P, KT, D])
        w1 = sb("w1", [P, F])
        w2 = sb("w2", [P, FT, D])
        kT = sb("kT", [P, B, M])
        khat = sb("khat", [P, B, H, M])
        vhat = sb("vhat", [P, B, 2, RT, HH, VC])
        mx = sb("mx", [P, 2, HH])
        mc = sb("mc", [P, 2, HH])
        zb = sb("zb", [P, 2, HALF])
        pb = sb("pb", [P, 2, PADW])
        ptb = sb("ptb", [P, 2, PADW])
        rden = sb("rden", [P, 2, H])
        on = sb("on", [P, 2, D])
        onT = sb("onT", [P, 2, D])
        rr = sb("rr", [P, TPB, D])
        st = sb("st", [P, TPB, 6])
        mv = sb("mv", [P, TPB, 2])
        ve = sb("ve", [P, TPB])
        rs = sb("rs", [P, TPB])
        mhalf = sb("mhalf", [P, TPB])
        x2T = yy
        ot = a1[:, 0:2 * TPB].rearrange("p (s t) d -> p s t d", t=TPB)
        hT = b1s[:].rearrange("p (s f) t -> p s f t", f=FT)

        ps = ctx.enter_context(nc.psum_tensor("ps", [P, 8, 512], F32))
        bank = [ps[:, i, :] for i in range(8)]

        ld = {n: sem(f"ld_{n}") for n in ("vec", "x0", "x1", "x2", "x3", "w", "kv", "bo", "lg", "a1",
                                          "b1a", "b1b", "b2", "a2a", "a2b", "id", "hm", "vm")}
        s_const = sem("const_ready")
        s_sp_e = sem("softplus_exp")
        s_sp_l = sem("softplus_ln")
        s_nsp = sem("neg_softplus_ready")
        s_lmax = sem("logit_max")
        s_lexp = sem("logit_exp")
        s_wsel = sem("primitive_weights")
        s_a1w = sem("a1_weighted")
        s_b2w = sem("b2_weighted")
        s_x1ps = sem("x1_in_psum")
        s_yps = sem("y_in_psum")
        s_x1 = sem("x1_ready")
        s_x2 = sem("conv_ready")
        s_gxps = sem("gate_x_in_psum")
        s_gaps = sem("gate_a_in_psum")
        s_gx = sem("gate_x_ready")
        s_ga = sem("gate_a_ready")
        s_y = sem("gelu_ready")
        s_u = sem("a_squared_ready")
        s_um = sem("a_squared_capped")
        s_a = sem("a_ready")
        s_a0 = sem("a_first_zeroed")
        s_mult = sem("multiplier_ready")
        s_mult0 = sem("multiplier_first_set")
        s_r1 = sem("r1_ready")
        s_r1ps = sem("r1_turned")
        s_x1n = sem("ln1_ready")
        s_x1tps = sem("ln1_turned")
        s_x1t = sem("ln1_channel_major")
        s_qps = sem("q_in_psum")
        s_q = sem("q_ready")
        s_kps = sem("k_in_psum")
        s_k = sem("k_ready")
        s_khat = sem("khat_ready")
        s_vps = sem("v_in_psum")
        s_vhat = sem("vhat_ready")
        s_w1ps = sem("w1_in_psum")
        s_w1 = sem("w1_ready")
        s_w2ps = sem("w2_in_psum")
        s_w2 = sem("w2_ready")
        s_sps = sem("scores_in_psum")
        s_z = sem("shifted_scores")
        s_zc = sem("capped_scores")
        s_p = sem("probs_ready")
        s_ptps = sem("probs_turned")
        s_pt = sem("turned_probs_ready")
        s_o = sem("attention_in_psum")
        s_on = sem("attention_normed")
        s_ontps = sem("attention_turned")
        s_ont = sem("turned_attention_ready")
        s_rps = sem("attention_out_in_psum")
        s_r2 = sem("r2_ready")
        s_var = sem("variance_ready")
        s_rstd = sem("rstd_ready")
        s_x2n = sem("ln2_ready")
        s_x2tps = sem("ln2_turned")
        s_x2t = sem("ln2_channel_major")
        s_hps = sem("hidden_in_psum")
        s_h = sem("hidden_ready")
        s_fps = sem("ffn_in_psum")
        s_r3 = sem("r3_ready")
        s_out = sem("output_ready")
        s_st = [sem(f"output_stored_{i}") for i in range(B)]
        s_dve = sem("vector_step")
        s_pool = sem("pool_step")

        block = ctx.enter_context(nc.Block())

        @block.sync
        def _(sp):
            sp.dma_start(vec[:], vecs).then_inc(ld["vec"], 16)
            sp.dma_start(w[:, 0:2], wpack[:, 0:2]).then_inc(ld["w"], 16)
            sp.dma_start(xc[:, 0], xT[:, 0]).then_inc(ld["x0"], 16)
            sp.wait_ge(ld["w"], 16)
            sp.dma_start(w[:, 2:6], wpack[:, 2:6]).then_inc(ld["w"], 16)
            for b in range(1, B):
                sp.dma_start(xc[:, b], xT[:, b]).then_inc(ld[f"x{b}"], 16)
            sp.dma_start(lg[:], logits.partition_broadcast(P)).then_inc(ld["lg"], 16)
            sp.dma_start(kvp[:], kvpack).then_inc(ld["kv"], 16)
            sp.dma_start(hm[:], hmask).then_inc(ld["hm"], 16)
            sp.dma_start(vm[:], vmask).then_inc(ld["vm"], 16)
            sp.dma_start(idn[:], ident).then_inc(ld["id"], 16)
            sp.dma_start(bo_row[:], bo).then_inc(ld["bo"], 16)
            sp.dma_start(a1[:], a1T).then_inc(ld["a1"], 16)
            sp.dma_start(b1s[:, 0:KT // 2], b1[:, 0:KT // 2]).then_inc(ld["b1a"], 16)
            sp.dma_start(b1s[:, KT // 2:], b1[:, KT // 2:]).then_inc(ld["b1b"], 16)
            sp.dma_start(b2s[:], b2).then_inc(ld["b2"], 16)
            sp.dma_start(a2[:, 0:KT // 2], a2T[:, 0:KT // 2]).then_inc(ld["a2a"], 16)
            sp.dma_start(a2[:, KT // 2:], a2T[:, KT // 2:]).then_inc(ld["a2b"], 16)
            for b in range(B):
                sp.wait_ge(s_out, b + 1)
                sp.dma_start(out[b].rearrange("(t p) d -> p t d", p=P), ot[:, b % 2]).then_inc(s_st[b], 16)
            for b in range(B):
                sp.wait_ge(s_st[b], 16)

        @block.tensor
        def _(pe):
            for b in range(B):
                if b == 0:
                    pe.wait_ge(ld["w"], 16)
                pe.wait_ge(ld[f"x{b}"], 16)
                if b >= 2:
                    pe.wait_ge(s_x1, b - 1)
                nc.tensor.matmul(bank[b % 2], w[:, W_X], xc[:, b], start=True, stop=True).then_inc(s_x1ps, 1)
                if b >= 2:
                    pe.wait_ge(s_y, b - 1)
                nc.tensor.matmul(bank[2 + b % 2], w[:, W_Y], xc[:, b], start=True, stop=True).then_inc(s_yps, 1)
            pe.wait_ge(ld["kv"], 16)
            ctxT = kvp[:, 0:B * 3 * M].rearrange("p (b r m) -> p b r m", b=B, r=3)
            ctxr = kvp[:, 0:B * 3 * M].rearrange("p (b m) -> p b m", b=B)
            wk = kvp[:, B * 3 * M:B * 3 * M + D]
            wv = kvp[:, B * 3 * M + D:]
            nc.tensor.matmul(bank[4][:, 0:B * M].rearrange("p (b m) -> p b m", b=B), wk, ctxT[:, :, 0, :],
                             start=True, stop=True).then_inc(s_kps, 1)
            pe.wait_ge(ld["w"], 32)
            for b in range(B):
                pe.wait_ge(s_x2, b + 1)
                if b == 0:
                    pe.wait_ge(s_x1, B)
                if b >= 2:
                    pe.wait_ge(s_gx, b - 1)
                nc.tensor.matmul(bank[b % 2], w[:, W_GI], x2[:, b], start=True, stop=True).then_inc(s_gxps, 1)
                if b == 0:
                    pe.wait_ge(s_y, B)
                if b >= 2:
                    pe.wait_ge(s_ga, b - 1)
                nc.tensor.matmul(bank[2 + b % 2], w[:, W_GA], x2[:, b], start=True, stop=True).then_inc(s_gaps, 1)
            for n in range(2 * B):
                b, f = divmod(n, 2)
                if n >= 2:
                    pe.wait_ge(s_vhat, n - 1)
                for i in range(RT):
                    at = (i * P) % M
                    last = nc.tensor.matmul(bank[5 + n % 2][:, i * HH * HD:(i + 1) * HH * HD],
                                            ctxr[:, b, at:at + P], wv[:, f * HH * HD:(f + 1) * HH * HD],
                                            start=True, stop=True)
                last.then_inc(s_vps, 1)
            pe.wait_ge(s_a1w, 1)
            for k in range(KT):
                if k % (KT // 2) == 0:
                    pe.wait_ge(ld["b1a" if k == 0 else "b1b"], 16)
                last = nc.tensor.matmul(bank[7], a1[:, k], b1s[:, k], start=(k == 0), stop=(k == KT - 1))
            last.then_inc(s_w1ps, 1)

            def w2_chunk(j):
                if j == 0:
                    pe.wait_ge(s_w1, 1)
                    pe.wait_ge(s_b2w, 1)
                    pe.wait_ge(ld["a2a"], 16)
                    pe.wait_ge(ld["a2b"], 16)
                else:
                    pe.wait_ge(s_w2, j)
                for k in range(KT):
                    mm = nc.tensor.matmul(bank[7][:, 0:D], a2[:, k, j * P:(j + 1) * P], b2s[:, k],
                                          start=(k == 0), stop=(k == KT - 1))
                mm.then_inc(s_w2ps, 1)

            pe.wait_ge(ld["id"], 16)
            for b in range(B):
                w2_chunk(b)
                pe.wait_ge(s_r1, b + 1)
                if b == 0:
                    pe.wait_ge(s_k, 1)
                    pe.wait_ge(s_vhat, 2 * B)
                if b >= 1:
                    pe.wait_ge(s_x1n, b)
                for i in range(TPB):
                    last = nc.tensor.transpose(bank[4][:, i * P:(i + 1) * P], xc[:, b, i * P:(i + 1) * P], idn[:])
                last.then_inc(s_r1ps, 1)
                pe.wait_ge(s_x1n, b + 1)
                if b >= 1:
                    pe.wait_ge(s_x1t, b)
                for i in range(TPB):
                    last = nc.tensor.transpose(bank[5][:, i * P:(i + 1) * P], x1n[:, b * TPB + i], idn[:])
                last.then_inc(s_x1tps, 1)
                pe.wait_ge(s_x1t, b + 1)
                if b >= 1:
                    pe.wait_ge(s_q, b)
                nc.tensor.matmul(bank[6], w[:, W_Q], x2[:, b], start=True, stop=True).then_inc(s_qps, 1)

            def scores(t, f):
                b = t // TPB
                n = 2 * t + f
                if n == 0:
                    pe.wait_ge(s_khat, 1)
                    pe.wait_ge(s_gx, B)
                    pe.wait_ge(s_ga, B)
                if f == 0:
                    pe.wait_ge(s_q, b + 1)
                if n >= 2:
                    pe.wait_ge(s_z, n - 1)
                for g in range(2):
                    h = f * HH + 4 * g
                    last = nc.tensor.matmul(bank[2 * f + g][:, 0:QUAD].rearrange("p (h m) -> p h m", h=4),
                                            qT[:, b, (t % TPB) * P:(t % TPB + 1) * P],
                                            khat[:, b, h:h + 4], start=True, stop=True)
                last.then_inc(s_sps, 1)

            def turn_probs(t, f):
                n = 2 * t + f
                pe.wait_ge(s_p, n + 1)
                if n == 0:
                    pe.wait_ge(s_x1t, B)
                    pe.wait_ge(s_x1n, B)
                if n >= 1:
                    pe.wait_ge(s_pt, n)
                for i in range(RT):
                    last = nc.tensor.transpose(bank[4 + i // 4][:, (i % 4) * P:(i % 4 + 1) * P],
                                               pb[:, f, i * P:(i + 1) * P], idn[:])
                last.then_inc(s_ptps, 1)

            def weigh_values(t, f):
                n = 2 * t + f
                pe.wait_ge(s_pt, n + 1)
                if n == 0:
                    pe.wait_ge(s_q, B)
                if f == 0 and t >= 1:
                    pe.wait_ge(s_on, t)
                for i in range(RT):
                    last = nc.tensor.matmul(bank[6][:, f * HH * VC:(f + 1) * HH * VC],
                                            ptb[:, f, i * P:(i + 1) * P],
                                            vhat[:, t // TPB, f, i].rearrange("p h c -> p (h c)"),
                                            start=(i == 0), stop=(i == RT - 1))
                last.then_inc(s_o, 1)

            def project(t):
                pe.wait_ge(s_on, t + 1)
                if t == 0:
                    pe.wait_ge(s_w2, FT)
                    pe.wait_ge(ld["bo"], 16)
                    pe.wait_ge(s_const, 3)
                if t >= 1:
                    pe.wait_ge(s_r2, t)
                nc.tensor.transpose(bank[7][:, 0:P], on[:, t % 2], idn[:]).then_inc(s_ontps, 1)
                pe.wait_ge(s_ont, t + 1)
                nc.tensor.matmul(bank[7][:, P:2 * P], onT[:, t % 2], w[:, W_O], start=True, stop=False)
                nc.tensor.matmul(bank[7][:, P:2 * P], ones_row[:], bo_row[:], start=False,
                                 stop=True).then_inc(s_rps, 1)

            for t in range(NT):
                for f in range(2):
                    scores(t, f)
                if t >= 1:
                    for f in range(2):
                        turn_probs(t - 1, f)
                        weigh_values(t - 1, f)
                    if t >= 2:
                        project(t - 2)
            for f in range(2):
                turn_probs(NT - 1, f)
                weigh_values(NT - 1, f)
            project(NT - 2)
            project(NT - 1)

            for b in range(B):
                pe.wait_ge(s_x2n, TPB * (b + 1))
                if b == 0:
                    pe.wait_ge(s_on, NT)
                if b >= 1:
                    pe.wait_ge(s_x2t, b)
                for i in range(TPB):
                    last = nc.tensor.transpose(bank[6][:, i * P:(i + 1) * P], x2n[:, b * TPB + i], idn[:])
                last.then_inc(s_x2tps, 1)
                pe.wait_ge(s_x2t, b + 1)
                for j in range(FT):
                    if b >= 1:
                        pe.wait_ge(s_h, FT * (b - 1) + j + 1)
                    nc.tensor.matmul(bank[j], w1[:, j * P:(j + 1) * P], x2T[:, b % 2], start=True,
                                     stop=True).then_inc(s_hps, 1)
                if b >= 2:
                    pe.wait_ge(s_r3, b - 1)
                pe.wait_ge(s_h, FT * (b + 1))
                for i in range(TPB):
                    for j in range(FT):
                        last = nc.tensor.matmul(bank[4 + b % 2][:, i * P:(i + 1) * P],
                                                hT[:, b % 2, j, i * P:(i + 1) * P], w2[:, j],
                                                start=(j == 0), stop=(j == FT - 1))
                last.then_inc(s_fps, 1)

        @block.scalar
        def _(act):
            def col(c):
                return vec[:, c:c + 1]

            act.wait_ge(s_nsp, 1)
            nc.scalar.activation(spt[:, 1:2], spt[:, 0:1], ACT.Exp, scale=-1.0).then_inc(s_sp_e, 1)
            act.wait_ge(s_sp_e, 1)
            nc.scalar.activation(spt[:, 2:3], spt[:, 1:2], ACT.Ln, bias=1.0).then_inc(s_sp_l, 1)
            act.wait_ge(s_lmax, 1)
            for i in range(2):
                last = nc.scalar.activation(lg[:, i], lg[:, i], ACT.Exp, bias=lgm[:, i:i + 1],
                                            accum_out=lgs[:, i:i + 1])
            last.then_inc(s_lexp, 1)
            act.wait_ge(s_const, 1)
            for b in range(B):
                act.wait_ge(s_x1ps, b + 1)
                nc.scalar.activation(x1p[:, b, TW - 1:], bank[b % 2], ACT.Identity, bias=col(V_BX)).then_inc(s_x1, 1)
                act.wait_ge(s_yps, b + 1)
                nc.scalar.activation(yy[:, b], bank[2 + b % 2], ACT.Gelu, bias=col(V_BY)).then_inc(s_y, 1)
            act.wait_ge(s_kps, 1)
            nc.scalar.activation(kT[:].rearrange("p b m -> p (b m)"), bank[4][:, 0:B * M], ACT.Identity,
                                 scale=SCALE).then_inc(s_k, 1)
            for b in range(B):
                act.wait_ge(s_gxps, b + 1)
                nc.scalar.activation(gx[:, b], bank[b % 2], ACT.Sigmoid, bias=col(V_GIB)).then_inc(s_gx, 1)
                act.wait_ge(s_gaps, b + 1)
                nc.scalar.activation(aa[:, b], bank[2 + b % 2], ACT.Sigmoid, bias=col(V_GAB)).then_inc(s_ga, 1)
            act.wait_ge(s_nsp, 2)
            for b in range(B):
                act.wait_ge(s_ga, b + 1)
                nc.scalar.activation(uu[:, b], aa[:, b], ACT.Exp, scale=spt[:, 5:6]).then_inc(s_u, 1)
                nc.scalar.activation(aa[:, b], aa[:, b], ACT.Exp, scale=spt[:, 4:5]).then_inc(s_a, 1)
            for b in range(B):
                act.wait_ge(s_um, b + 1)
                nc.scalar.activation(uu[:, b], uu[:, b], ACT.Sqrt, scale=-1.0, bias=1.0).then_inc(s_mult, 1)
            act.wait_ge(s_w1ps, 1)
            nc.scalar.copy(w1[:], bank[7]).then_inc(s_w1, 1)
            for b in range(B):
                act.wait_ge(s_w2ps, b + 1)
                nc.scalar.copy(w2[:, b], bank[7][:, 0:D]).then_inc(s_w2, 1)
                act.wait_ge(s_x1tps, b + 1)
                nc.scalar.copy(x2[:, b], bank[5]).then_inc(s_x1t, 1)
                act.wait_ge(s_qps, b + 1)
                nc.scalar.activation(qT[:, b], bank[6], ACT.Identity, bias=col(V_BQ)).then_inc(s_q, 1)

            def probs(t, f):
                n = 2 * t + f
                act.wait_ge(s_zc, n + 1)
                if n >= 2:
                    act.wait_ge(s_ptps, n - 1)
                nc.scalar.activation(pb[:, f, 0:HALF], zb[:, f], ACT.Exp).then_inc(s_p, 1)

            def take_probs(t, f):
                n = 2 * t + f
                act.wait_ge(s_ptps, n + 1)
                if n >= 2:
                    act.wait_ge(s_o, n - 1)
                nc.scalar.copy(ptb[:, f], ps[:, 4:6, :].rearrange("p a c -> p (a c)")[:, 0:PADW]).then_inc(s_pt, 1)

            def take_attention(t):
                act.wait_ge(s_ontps, t + 1)
                if t >= 2:
                    act.wait_ge(s_rps, t - 1)
                nc.scalar.copy(onT[:, t % 2], bank[7][:, 0:P]).then_inc(s_ont, 1)

            for t in range(NT):
                if t >= 1:
                    for f in range(2):
                        take_probs(t - 1, f)
                if t >= 2:
                    take_attention(t - 2)
                for f in range(2):
                    probs(t, f)
            for f in range(2):
                take_probs(NT - 1, f)
            take_attention(NT - 2)
            take_attention(NT - 1)
            for b in range(B):
                act.wait_ge(s_x2tps, b + 1)
                if b >= 2:
                    act.wait_ge(s_hps, FT * (b - 1))
                nc.scalar.copy(x2T[:, b % 2], bank[6]).then_inc(s_x2t, 1)
                if b >= 2:
                    act.wait_ge(s_fps, b - 1)
                for j in range(FT):
                    act.wait_ge(s_hps, FT * b + j + 1)
                    nc.scalar.activation(hT[:, b % 2, j], bank[j], ACT.Gelu_apprx_tanh).then_inc(s_h, 1)

        @block.vector
        def _(dve):
            steps = [0]

            def step(ins):
                steps[0] += 1
                ins.then_inc(s_dve, 1)
                dve.wait_ge(s_dve, steps[0])

            v = nc.vector
            step(v.memset(ones_row[:], 1.0))
            v.memset(mhalf[:], -0.5).then_inc(s_const, 1)
            dve.wait_ge(ld["vec"], 16)
            step(v.tensor_scalar(spt[:, 6:7], vec[:, V_AP:V_AP + 1], -1.0, None, ALU.mult))
            v.tensor_tensor(spt[:, 0:1], spt[:, 6:7], vec[:, V_AP:V_AP + 1], ALU.max).then_inc(s_nsp, 1)
            dve.wait_ge(ld["lg"], 16)
            step(v.tensor_reduce(lgm[:], lg[:], AX_X, ALU.max))
            v.tensor_scalar(lgm[:], lgm[:], -1.0, None, ALU.mult).then_inc(s_lmax, 1)
            dve.wait_ge(s_sp_l, 1)
            step(v.scalar_tensor_tensor(spt[:, 3:4], vec[:, V_AP:V_AP + 1], 0.0, spt[:, 2:3], ALU.max, ALU.add))
            step(v.tensor_scalar(spt[:, 4:5], spt[:, 3:4], -C_GATE, None, ALU.mult))
            v.tensor_scalar(spt[:, 5:6], spt[:, 3:4], -2.0 * C_GATE, None, ALU.mult).then_inc(s_nsp, 1)
            dve.wait_ge(s_lexp, 1)
            step(v.reciprocal(lgs[:], lgs[:]))
            hp = P // 2
            for i in range(2):
                for q in range(2):
                    last = v.tensor_scalar(wsel[q * hp:(q + 1) * hp, i],
                                           lg[q * hp:(q + 1) * hp, i].rearrange("p (k q) -> p q k", q=2)[:, q],
                                           lgs[q * hp:(q + 1) * hp, i:i + 1], None, ALU.mult)
            last.then_inc(s_wsel, 1)
            for b in range(B):
                dve.wait_ge(s_x1, b + 1)
                if b == 0:
                    dve.wait_ge(s_const, 3)
                step(v.tensor_scalar(x2[:, b], x1p[:, b, 0:T], vec[:, V_CW:V_CW + 1], vec[:, V_CB:V_CB + 1],
                                     ALU.mult, ALU.add))
                for i in range(1, TW):
                    ins = v.scalar_tensor_tensor(x2[:, b], x1p[:, b, i:i + T], vec[:, V_CW + i:V_CW + i + 1],
                                                 x2[:, b], ALU.mult, ALU.add)
                    if i < TW - 1:
                        step(ins)
                ins.then_inc(s_x2, 1)
            dve.wait_ge(s_wsel, 1)
            dve.wait_ge(ld["a1"], 16)
            v.tensor_tensor(a1[:], a1[:], wsel[:, 0, :].unsqueeze(2).to_broadcast([P, KT, D]),
                            ALU.mult).then_inc(s_a1w, 1)
            dve.wait_ge(ld["vm"], 16)
            for n in range(2 * B):
                b, f = divmod(n, 2)
                dve.wait_ge(s_vps, n + 1)
                v.tensor_copy(vhat[:, b, f, :, :, HD:VC], vm[:].unsqueeze(3))
                v.tensor_tensor(vhat[:, b, f, :, :, 0:HD].rearrange("p i h c -> p (i h) c"),
                                bank[5 + n % 2][:, 0:RT * HH * HD].rearrange("p (n c) -> p n c", c=HD),
                                vm[:].rearrange("p i h -> p (i h)").unsqueeze(2).to_broadcast([P, RT * HH, HD]),
                                ALU.mult).then_inc(s_vhat, 1)
            for b in range(B):
                dve.wait_ge(s_gx, b + 1)
                step(v.tensor_tensor(gx[:, b], gx[:, b], x2[:, b], ALU.mult))
                dve.wait_ge(s_u, b + 1)
                v.tensor_scalar(uu[:, b], uu[:, b], 1.0, None, ALU.min).then_inc(s_um, 1)
            for b in range(B):
                dve.wait_ge(s_mult, b + 1)
                step(v.memset(uu[:, b, 0:1], 1.0))
                step(v.tensor_tensor(gx[:, b], gx[:, b], uu[:, b], ALU.mult))
                dve.wait_ge(s_a, b + 1)
                step(v.memset(aa[:, b, 0:1], 0.0))
                step(v.tensor_tensor_scan(uu[:, b], aa[:, b], gx[:, b], 0.0, ALU.mult, ALU.add))
                dve.wait_ge(s_y, b + 1)
                step(v.tensor_tensor(yy[:, b], yy[:, b], uu[:, b], ALU.mult))
                v.tensor_tensor(xc[:, b], xc[:, b], yy[:, b], ALU.add).then_inc(s_r1, 1)

            def norm_tiles(src, dst, n0, n):
                for i in range(n):
                    step(v.bn_stats(st[:, i], src(i)))
                    step(v.bn_aggr(mv[:, i], st[:, i]))
                v.tensor_scalar(ve[:, 0:n], mv[:, 0:n, 1], EPS, None, ALU.add).then_inc(s_var, 1)
                dve.wait_ge(s_rstd, n0 + 1)
                for i in range(n):
                    last = v.tensor_scalar(dst(i), src(i), mv[:, i, 0:1], rs[:, i:i + 1], ALU.subtract, ALU.mult)
                return last

            for b in range(B):
                dve.wait_ge(s_r1ps, b + 1)
                norm_tiles(lambda i: bank[4][:, i * P:(i + 1) * P], lambda i: x1n[:, b * TPB + i], b,
                           TPB).then_inc(s_x1n, 1)

            def soft(t, f):
                n = 2 * t + f
                dve.wait_ge(s_sps, n + 1)
                s = ps[:, 2 * f:2 * f + 2, 0:QUAD]
                step(v.tensor_reduce(mx[:, f], s.rearrange("p g (h m) -> p g h m", m=M), AX_X, ALU.max))
                step(v.tensor_scalar(mc[:, f], mx[:, f], CLAMP, -CLAMP, ALU.min, ALU.max))
                if n >= 2:
                    dve.wait_ge(s_p, n - 1)
                v.scalar_tensor_tensor(zb[:, f].rearrange("p (g c) -> p g c", g=2), s, -CLAMP,
                                       mc[:, f].unsqueeze(2).to_broadcast([P, HH, M]),
                                       ALU.max, ALU.subtract).then_inc(s_z, 1)

            def norm_heads(t):
                dve.wait_ge(s_o, 2 * (t + 1))
                if t >= 2:
                    dve.wait_ge(s_ontps, t - 1)
                o = bank[6][:, 0:H * VC].rearrange("p (h c) -> p h c", c=VC)
                step(v.reciprocal(rden[:, t % 2], o[:, :, HD]))
                v.tensor_tensor(on[:, t % 2].rearrange("p (h c) -> p h c", c=HD), o[:, :, 0:HD],
                                rden[:, t % 2].unsqueeze(2).to_broadcast([P, H, HD]), ALU.mult).then_inc(s_on, 1)

            def ln2(t):
                dve.wait_ge(s_rps, t + 1)
                if t >= 1:
                    dve.wait_ge(s_x2n, t)
                ins = v.tensor_tensor(rr[:, 0], bank[7][:, P:2 * P], x1n[:, t], ALU.add)
                ins.then_inc(s_r2, 1)
                dve.wait_ge(s_r2, t + 1)
                norm_tiles(lambda i: rr[:, 0], lambda i: x2n[:, t], B + t, 1).then_inc(s_x2n, 1)

            for t in range(NT):
                for f in range(2):
                    soft(t, f)
                if t >= 1:
                    norm_heads(t - 1)
                if t >= 2:
                    ln2(t - 2)
            norm_heads(NT - 1)
            ln2(NT - 2)
            ln2(NT - 1)
            for b in range(B):
                dve.wait_ge(s_fps, b + 1)
                if b == 0:
                    dve.wait_ge(s_x2n, NT)
                else:
                    dve.wait_ge(s_out, b)
                ins = v.tensor_tensor(rr[:].rearrange("p t d -> p (t d)"), bank[4 + b % 2],
                                      x2n[:, b * TPB:(b + 1) * TPB].rearrange("p t d -> p (t d)"), ALU.add)
                ins.then_inc(s_r3, 1)
                dve.wait_ge(s_r3, b + 1)
                if b >= 2:
                    dve.wait_ge(s_st[b - 2], 16)
                norm_tiles(lambda i: rr[:, i], lambda i: ot[:, b % 2, i], B + NT + b, TPB).then_inc(s_out, 1)

        @block.gpsimd
        def _(pool):
            g = nc.gpsimd
            g.memset(x1p[:, :, 0:TW - 1], 0.0).then_inc(s_const, 1)
            g.memset(pb[:, :, HALF:PADW], 0.0).then_inc(s_const, 1)
            pool.wait_ge(s_k, 1)
            pool.wait_ge(ld["hm"], 16)
            for b in range(B):
                last = g.tensor_tensor(khat[:, b], kT[:, b].unsqueeze(1).to_broadcast([P, H, M]),
                                       hm[:].unsqueeze(2).to_broadcast([P, H, M]), ALU.mult)
            last.then_inc(s_khat, 1)
            pool.wait_ge(s_wsel, 1)
            pool.wait_ge(ld["b2"], 16)
            g.tensor_tensor(b2s[:], b2s[:], wsel[:, 1, :].unsqueeze(2).to_broadcast([P, KT, D]),
                            ALU.mult).then_inc(s_b2w, 1)

            def root(n, width):
                pool.wait_ge(s_var, n + 1)
                g.tensor_tensor(rs[:, 0:width], ve[:, 0:width], mhalf[:, 0:width], ALU.pow).then_inc(s_rstd, 1)

            for b in range(B):
                root(b, TPB)
            for t in range(NT):
                for f in range(2):
                    n = 2 * t + f
                    pool.wait_ge(s_z, n + 1)
                    g.tensor_scalar(zb[:, f], zb[:, f], 0.0, -2.0 * CLAMP, ALU.min, ALU.max).then_inc(s_zc, 1)
                if t >= 2:
                    root(B + t - 2, 1)
            root(B + NT - 2, 1)
            root(B + NT - 1, 1)
            for b in range(B):
                root(B + NT + b, TPB)


def kernel(x, ctx_768, L0_attn_w_x, L0_attn_b_x, L0_attn_w_y, L0_attn_b_y, L0_attn_conv_w, L0_attn_conv_b,
           L0_attn_gi_w, L0_attn_gi_b, L0_attn_ga_w, L0_attn_ga_b, L0_attn_a_param, L0_xattn_Wq, L0_xattn_bq,
           L0_xattn_Wk, L0_xattn_bk, L0_xattn_Wv, L0_xattn_bv, L0_xattn_Wo, L0_xattn_bo, L0_ffn_fc1_A,
           L0_ffn_fc1_B, L0_ffn_fc2_A, L0_ffn_fc2_B, L0_ffn_fc1_logits, L0_ffn_fc2_logits):
    import concourse.bacc as bacc
    from concourse.bass_utils import run_bass_kernel_spmd

    c = np.ascontiguousarray
    a = {}
    a["xT"] = c(np.transpose(x, (2, 0, 1)))
    a["vecs"] = c(np.stack([*L0_attn_conv_w, L0_attn_b_x, L0_attn_b_y, L0_attn_conv_b, L0_attn_gi_b,
                            L0_attn_ga_b, L0_attn_a_param, L0_xattn_bq], axis=1))
    a["wpack"] = c(np.stack([L0_attn_w_x, L0_attn_w_y, L0_attn_gi_w, L0_attn_ga_w, L0_xattn_Wq, L0_xattn_Wo],
                            axis=1))
    ctxT = np.transpose(ctx_768, (2, 0, 1))
    ctxT = np.concatenate([ctxT, ctxT, ctxT], axis=2).reshape(DC, B * 3 * M)
    ctxT = np.concatenate([ctxT, np.ones((1, B * 3 * M), np.float32)], axis=0)
    wkv = np.concatenate([np.concatenate([L0_xattn_Wk, L0_xattn_bk[None]], axis=0),
                          np.concatenate([L0_xattn_Wv, L0_xattn_bv[None]], axis=0)], axis=1)
    a["kvpack"] = c(np.concatenate([ctxT, wkv], axis=1))
    a["bo"] = c(L0_xattn_bo[None])
    a["logits"] = c(np.stack([L0_ffn_fc1_logits, L0_ffn_fc2_logits]))
    a["a1T"] = c(np.transpose(np.transpose(L0_ffn_fc1_A, (0, 2, 1)).reshape(KT, P, D), (1, 0, 2)))
    a["b1"] = c(np.transpose(L0_ffn_fc1_B.reshape(KT, P, F), (1, 0, 2)))
    a["a2T"] = c(np.transpose(np.transpose(L0_ffn_fc2_A, (0, 2, 1)).reshape(KT, P, F), (1, 0, 2)))
    a["b2"] = c(np.transpose(L0_ffn_fc2_B.reshape(KT, P, D), (1, 0, 2)))
    a["ident"] = np.eye(P, dtype=np.float32)
    a["hmask"] = np.repeat(np.eye(H, dtype=np.float32), HD, axis=0)
    row = np.arange(PADW)
    a["vmask"] = c(np.transpose((row[:, None] // M == np.arange(HH)[None]).astype(np.float32).reshape(RT, P, HH),
                                (1, 0, 2)))
    nc = bacc.Bacc("TRN2", target_bir_lowering=False, num_devices=1)
    names = ["xT", "vecs", "wpack", "kvpack", "bo", "logits", "a1T", "b1", "a2T", "b2", "ident", "hmask", "vmask"]
    arrays = {f"in_{n}": a[n] for n in names}
    args = [nc.dram_tensor(f"in_{n}", a[n].shape, F32, kind="ExternalInput").ap() for n in names]
    out = nc.dram_tensor("out", (B, T, D), F32, kind="ExternalOutput").ap()
    build(nc, *args, out)
    r = run_bass_kernel_spmd(nc, [arrays], core_ids=[0])
    return r.results[0]["out"]
```

```python
from contextlib import ExitStack

import numpy as np

import concourse.bass as bass
from concourse import mybir

ALU = mybir.AluOpType
ACT = mybir.ActivationFunctionType
F32 = mybir.dt.float32
F32R = mybir.dt.float32r
AX_X = mybir.AxisListType.X

P = 128
B, T, D = 4, 512, 128
TPB = T // P
NT = B * TPB
M, DC = 77, 96
H = 16
HD = D // H
HH = H // 2
HALF = HH * M
NG = H // 4
QUAD = 4 * M
RT = -(-HALF // P)
PADW = RT * P
VC = HD + 1
NP_, R, F = 32, 64, 512
KT = NP_ * R // P
FT = F // P
TW = 4
C_GATE = 8.0
CLAMP = 10000.0
SCALE = float(HD) ** -0.5
EPS = 1e-5

V_CW, V_BX, V_BY, V_CB, V_GIB, V_GAB, V_AP, V_BQ, V_BO, V_N = 0, 4, 5, 6, 7, 8, 9, 10, 11, 12
W_X, W_Y, W_GI, W_GA, W_Q, W_O = range(6)


def build(nc, xT, vecs, wpack, kvpack, logits, a1T, b1, a2T, b2, ident, hmask, vmask, out):
    with ExitStack() as ctx:
        def sb(name, shape, dt=F32):
            return ctx.enter_context(nc.sbuf_tensor(name, shape, dt))

        def sem(name):
            return ctx.enter_context(nc.semaphore(name))

        xc = sb("xc", [P, B, T])
        x1p = sb("x1p", [P, B, T + TW - 1])
        x2 = sb("x2", [P, B, T])
        gx = sb("gx", [P, B, T])
        aa = sb("aa", [P, B, T])
        uu = sb("uu", [P, B, T])
        yy = sb("yy", [P, B, T])
        x1n = x1p[:].rearrange("p b t -> p (b t)")[:, 0:NT * D].rearrange("p (n d) -> p n d", d=D)
        x2n = aa[:].rearrange("p b (t d) -> p (b t) d", d=D)
        x2T = yy
        vec = sb("vec", [P, V_N])
        w = sb("w", [P, 6, D])
        kvp = sb("kvp", [DC + 1, B * 3 * M + 2 * D])
        idn = sb("idn", [P, P])
        hm = sb("hm", [P, 4])
        vm = sb("vm", [P, RT, HH])
        lg = sb("lg", [P, 2, NP_])
        lgm = sb("lgm", [P, 2])
        lgs = sb("lgs", [P, 2])
        wsel = sb("wsel", [P, 2, KT])
        spt = sb("spt", [P, 8])
        a1 = sb("a1", [P, KT, D])
        b1s = sb("b1s", [P, KT, F])
        a2 = sb("a2", [P, KT, F])
        b2s = sb("b2s", [P, KT, D])
        w1 = sb("w1", [P, F])
        w2 = sb("w2", [P, FT, D])
        kh = sb("kh", [P, B * M], F32R)
        kl = sb("kl", [P, B * M], F32R)
        qh = sb("qh", [P, 2, T], F32R)
        ql = sb("ql", [P, 2, T], F32R)
        qs = sb("qs", [P, 2, NG, T], F32R)
        ks = sb("ks", [P, B, NG, QUAD], F32R)
        vhat = sb("vhat", [P, B, 2, RT, HH, VC])
        z2 = a1[:].rearrange("p k d -> p (k d)")
        late = b1s[:, KT // 2:].rearrange("p k f -> p (k f)")
        zb = [late[:, 0:H * M], z2[:, 0:H * M]]
        pb = late[:, H * M:H * M + 2 * PADW].rearrange("p (f c) -> p f c", f=2)
        ptb = late[:, H * M + 2 * PADW:H * M + 4 * PADW].rearrange("p (f c) -> p f c", f=2)
        mx = sb("mx", [P, H])
        mc = sb("mc", [P, H])
        rden = sb("rden", [P, 2, H])
        st = sb("st", [P, 2, TPB, 6])
        mv = sb("mv", [P, 2, TPB, 2])
        ve = sb("ve", [P, 2, TPB])
        rs = sb("rs", [P, 2, TPB])
        nb = sb("nb", [P, 2, TPB])
        st3 = sb("st3", [P, TPB, 6])
        mv3 = sb("mv3", [P, TPB, 2])
        ve3 = sb("ve3", [P, TPB])
        rs3 = sb("rs3", [P, TPB])
        mhalf = sb("mhalf", [P, TPB])
        KSR0 = B * (T + TW - 1) - NG * B * M
        ksr = x1p[:].rearrange("p b t -> p (b t)")[:, KSR0:].rearrange("p (g c) -> p g c", g=NG)
        ot = a1[:, 0:2 * TPB].rearrange("p (s t) d -> p s t d", t=TPB)
        rr = a1[:, 2 * TPB:3 * TPB]
        on = a1[:, 3 * TPB:3 * TPB + 2]
        onT = a1[:, 3 * TPB + 2:4 * TPB]
        hT = b1s[:, 0:2 * FT].rearrange("p (s f) t -> p s f t", f=FT)

        ps = ctx.enter_context(nc.psum_tensor("ps", [P, 8, 512], F32))
        bank = [ps[:, i, :] for i in range(8)]
        flat = ps[:].rearrange("p a c -> p (a c)")
        SC = flat[:, 0:H * M]
        PT = flat[:, 3 * 512:3 * 512 + PADW]
        TA = H * VC
        OB, MB, FB = bank[5], bank[6], bank[7]

        ld = {n: sem(f"ld_{n}") for n in ("vec", "x0", "x1", "x2", "x3", "w", "w2", "kv", "lg", "a1",
                                          "b1a", "b1b", "b2", "a2a", "a2b", "id", "hm", "vm")}
        s_const = sem("const_ready")
        s_abs = sem("abs_a_param")
        s_sp_e = sem("softplus_exp")
        s_sp_l = sem("softplus_ln")
        s_nsp = sem("neg_softplus_ready")
        s_lmax = sem("logit_max")
        s_lexp = sem("logit_exp")
        s_wsel = sem("primitive_weights")
        s_a1w = sem("a1_weighted")
        s_b2w = sem("b2_weighted")
        s_x1ps = sem("x1_in_psum")
        s_yps = sem("y_in_psum")
        s_x1 = sem("x1_ready")
        s_tap0 = sem("first_tap_ready")
        s_x2 = sem("conv_ready")
        s_gxps = sem("gate_x_in_psum")
        s_gaps = sem("gate_a_in_psum")
        s_gx = sem("gate_x_ready")
        s_ga = sem("gate_a_ready")
        s_y = sem("gelu_ready")
        s_u = sem("a_squared_ready")
        s_um = sem("one_less_a_squared")
        s_a = sem("a_ready")
        s_mult = sem("multiplier_ready")
        s_r1 = sem("r1_ready")
        s_r1ps = sem("r1_turned")
        s_x1n = sem("ln1_ready")
        s_x1tps = sem("ln1_turned")
        s_x1t = sem("ln1_channel_major")
        s_x1b = sem("ln1_with_bo")
        s_qps = sem("q_in_psum")
        s_qh = sem("q_high_ready")
        s_ql = sem("q_low_ready")
        s_qs = [sem(f"q_stacked_{i}") for i in range(2)]
        s_kps = sem("k_in_psum")
        s_kh = sem("k_high_ready")
        s_kl = sem("k_low_ready")
        s_kst = sem("k_stacked")
        s_ks = sem("k_heads_apart")
        s_vps = sem("v_in_psum")
        s_vhat = sem("vhat_ready")
        s_w1ps = sem("w1_in_psum")
        s_w1 = sem("w1_ready")
        s_w2ps = sem("w2_in_psum")
        s_w2 = sem("w2_ready")
        s_sps = sem("scores_in_psum")
        s_z = sem("shifted_scores")
        s_zc = sem("capped_scores")
        s_p = sem("probs_ready")
        s_ptps = sem("probs_turned")
        s_pt = sem("turned_probs_ready")
        s_o = sem("attention_in_psum")
        s_on = sem("attention_normed")
        s_ontps = sem("attention_turned")
        s_ont = sem("turned_attention_ready")
        s_rps = sem("r2_in_psum")
        s_var = sem("variance_ready")
        s_rstd = sem("rstd_ready")
        s_x2n = sem("ln2_ready")
        s_x2tps = sem("ln2_turned")
        s_x2t = sem("ln2_channel_major")
        s_hps = sem("hidden_in_psum")
        s_h = sem("hidden_ready")
        s_fps = sem("ffn_in_psum")
        s_r3 = sem("r3_ready")
        s_out = sem("output_ready")
        s_st = [sem(f"output_stored_{i}") for i in range(B)]
        s_var3 = sem("variance3_ready")
        s_rstd3 = sem("rstd3_ready")
        s_gin = sem("gated_input")
        s_pad = sem("probs_padding_zeroed")
        s_st2 = sem("ln2_statistics")
        s_dve = sem("vector_step")
        s_pool = sem("pool_step")

        block = ctx.enter_context(nc.Block())

        SLOTS = NT + 3

        @block.sync
        def _(sp):
            sp.dma_start(w[:, 0:2], wpack[:, 0:2]).then_inc(ld["w"], 16)
            sp.dma_start(xc[:, 0], xT[:, 0]).then_inc(ld["x0"], 16)
            sp.dma_start(vec[:], vecs).then_inc(ld["vec"], 16)
            sp.dma_start(lg[:], logits.partition_broadcast(P)).then_inc(ld["lg"], 16)
            for b in range(1, B):
                sp.dma_start(xc[:, b], xT[:, b]).then_inc(ld[f"x{b}"], 16)
            sp.dma_start(w[:, 2:6], wpack[:, 2:6]).then_inc(ld["w2"], 16)
            sp.dma_start(kvp[:], kvpack).then_inc(ld["kv"], 16)
            sp.dma_start(vm[:], vmask).then_inc(ld["vm"], 16)
            sp.dma_start(hm[:], hmask).then_inc(ld["hm"], 16)
            sp.dma_start(a1[:], a1T).then_inc(ld["a1"], 16)
            sp.dma_start(idn[:], ident).then_inc(ld["id"], 16)
            sp.dma_start(b1s[:, 0:KT // 2], b1[:, 0:KT // 2]).then_inc(ld["b1a"], 16)
            sp.dma_start(b1s[:, KT // 2:], b1[:, KT // 2:]).then_inc(ld["b1b"], 16)
            sp.wait_ge(s_kh, 1)
            sp.wait_ge(s_kl, 1)
            sp.wait_ge(s_x2, B)
            for i, part in enumerate((kh, kl, kh, kl)):
                for g in range(NG):
                    sp.dma_start(ksr[32 * i:32 * i + 32, g], part[32 * g:32 * g + 32].bitcast(F32)).then_inc(s_kst, 16)
            sp.dma_start(b2s[:], b2).then_inc(ld["b2"], 16)
            sp.dma_start(a2[:, 0:KT // 2], a2T[:, 0:KT // 2]).then_inc(ld["a2a"], 16)
            sp.dma_start(a2[:, KT // 2:], a2T[:, KT // 2:]).then_inc(ld["a2b"], 16)
            for b in range(B):
                sp.wait_ge(s_qh, b + 1)
                sp.wait_ge(s_ql, b + 1)
                if b >= 2:
                    sp.wait_ge(s_sps, TPB * (b - 1))
                for i, part in enumerate((qh, qh, ql, ql)):
                    for g in range(NG):
                        sp.dma_start(qs[32 * i:32 * i + 32, b % 2, g].bitcast(F32),
                                     part[32 * g:32 * g + 32, b % 2].bitcast(F32)).then_inc(s_qs[b % 2], 16)
            for b in range(B):
                sp.wait_ge(s_out, b + 1)
                sp.dma_start(out[b].rearrange("(t p) d -> p t d", p=P), ot[:, b % 2]).then_inc(s_st[b], 16)
            for b in range(B):
                sp.wait_ge(s_st[b], 16)

        @block.tensor
        def _(pe):
            mm = nc.tensor.matmul
            pe.wait_ge(ld["w"], 16)
            for b in range(B):
                pe.wait_ge(ld[f"x{b}"], 16)
                if b >= 2:
                    pe.wait_ge(s_x1, b - 1)
                mm(bank[b % 2], w[:, W_X], xc[:, b], start=True, stop=True).then_inc(s_x1ps, 1)
                if b >= 2:
                    pe.wait_ge(s_y, b - 1)
                mm(bank[2 + b % 2], w[:, W_Y], xc[:, b], start=True, stop=True).then_inc(s_yps, 1)
            pe.wait_ge(ld["kv"], 16)
            ctxT = kvp[:, 0:B * 3 * M].rearrange("p (b r m) -> p b r m", b=B, r=3)
            ctxr = kvp[:, 0:B * 3 * M].rearrange("p (b m) -> p b m", b=B)
            wk = kvp[:, B * 3 * M:B * 3 * M + D]
            wv = kvp[:, B * 3 * M + D:]
            mm(bank[4][:, 0:B * M].rearrange("p (b m) -> p b m", b=B), wk, ctxT[:, :, 0, :],
               start=True, stop=True).then_inc(s_kps, 1)
            pe.wait_ge(ld["w2"], 16)
            for b in range(B):
                for f in range(2):
                    n = 2 * b + f
                    if n >= 2:
                        pe.wait_ge(s_vhat, n - 1)
                    for i in range(RT):
                        at = (i * P) % M
                        last = mm(bank[5 + n % 2][:, i * HH * HD:(i + 1) * HH * HD], ctxr[:, b, at:at + P],
                                  wv[:, f * HH * HD:(f + 1) * HH * HD], start=True, stop=True)
                    last.then_inc(s_vps, 1)
                pe.wait_ge(s_x2, b + 1)
                if b == 0:
                    pe.wait_ge(s_x1, B)
                if b >= 2:
                    pe.wait_ge(s_gx, b - 1)
                mm(bank[b % 2], w[:, W_GI], x2[:, b], start=True, stop=True).then_inc(s_gxps, 1)
                if b == 0:
                    pe.wait_ge(s_y, B)
                if b >= 2:
                    pe.wait_ge(s_ga, b - 1)
                mm(bank[2 + b % 2], w[:, W_GA], x2[:, b], start=True, stop=True).then_inc(s_gaps, 1)
            pe.wait_ge(s_a1w, 1)
            for k in range(KT):
                if k % (KT // 2) == 0:
                    pe.wait_ge(ld["b1a" if k == 0 else "b1b"], 16)
                last = mm(FB, a1[:, k], b1s[:, k], start=(k == 0), stop=(k == KT - 1))
            last.then_inc(s_w1ps, 1)

            def w2_part(t):
                j, q = divmod(t, 4)
                if t == 0:
                    pe.wait_ge(s_w1, 1)
                    pe.wait_ge(s_b2w, 1)
                    pe.wait_ge(ld["a2a"], 16)
                    pe.wait_ge(ld["a2b"], 16)
                elif q == 0:
                    pe.wait_ge(s_w2, j)
                for k in range(q * KT // 4, (q + 1) * KT // 4):
                    last = mm(FB[:, 0:D], a2[:, k, j * P:(j + 1) * P], b2s[:, k], start=(k == 0), stop=(k == KT - 1))
                if q == 3:
                    last.then_inc(s_w2ps, 1)

            def turn_r1(b):
                pe.wait_ge(s_r1, b + 1)
                if b == 0:
                    pe.wait_ge(ld["id"], 16)
                    pe.wait_ge(s_ga, B)
                    pe.wait_ge(s_kh, 1)
                    pe.wait_ge(s_kl, 1)
                if b >= 2:
                    pe.wait_ge(s_x1n, b - 1)
                for i in range(TPB):
                    last = nc.tensor.transpose(bank[3 + b % 2][:, i * P:(i + 1) * P],
                                               xc[:, b, i * P:(i + 1) * P], idn[:])
                last.then_inc(s_r1ps, 1)

            def turn_ln1(b):
                pe.wait_ge(s_x1n, b + 1)
                if b == 0:
                    pe.wait_ge(s_vhat, 2 * B)
                if b >= 1:
                    pe.wait_ge(s_x1b, b)
                for i in range(TPB):
                    last = nc.tensor.transpose(OB[:, i * P:(i + 1) * P], x1n[:, b * TPB + i], idn[:])
                last.then_inc(s_x1tps, 1)

            def project_q(b):
                pe.wait_ge(s_x1t, b + 1)
                if b >= 1:
                    pe.wait_ge(s_ql, b)
                mm(MB, w[:, W_Q], x2[:, b], start=True, stop=True).then_inc(s_qps, 1)

            turn_r1(0)
            turn_r1(1)
            for b in range(B):
                turn_ln1(b)
                project_q(b)
                if b + 2 < B:
                    turn_r1(b + 2)

            def scores(t):
                b = t // TPB
                if t == 0:
                    pe.wait_ge(s_ks, 1)
                    pe.wait_ge(s_gx, B)
                if t % TPB == 0:
                    pe.wait_ge(s_qs[b % 2], 16 * 4 * NG * (b // 2 + 1))
                if t >= 1:
                    pe.wait_ge(s_z, t)
                for g in range(NG):
                    lo = g * QUAD
                    while lo < (g + 1) * QUAD:
                        hi = min((g + 1) * QUAD, (lo // 512 + 1) * 512)
                        last = mm(SC[:, lo:hi], qs[:, b % 2, g, (t % TPB) * P:(t % TPB + 1) * P],
                                  ks[:, b, g, lo - g * QUAD:hi - g * QUAD], start=True, stop=True)
                        lo = hi
                last.then_inc(s_sps, 1)

            def turn_probs(t, f):
                n = 2 * t + f
                pe.wait_ge(s_p, n + 1)
                if n == 0:
                    pe.wait_ge(s_x1n, B)
                    pe.wait_ge(s_pad, 1)
                else:
                    pe.wait_ge(s_pt, n)
                for i in range(RT):
                    last = nc.tensor.transpose(PT[:, i * P:(i + 1) * P], pb[:, f, i * P:(i + 1) * P], idn[:])
                last.then_inc(s_ptps, 1)

            def weigh_values(t, f):
                pe.wait_ge(s_pt, 2 * t + f + 1)
                if t == 0 and f == 0:
                    pe.wait_ge(s_x1b, B)
                if t >= 1 and f == 0:
                    pe.wait_ge(s_on, t)
                    pe.wait_ge(s_ont, t)
                for i in range(RT):
                    last = mm(OB[:, f * HH * VC:(f + 1) * HH * VC], ptb[:, f, i * P:(i + 1) * P],
                              vhat[:, t // TPB, f, i].rearrange("p h c -> p (h c)"),
                              start=(i == 0), stop=(i == RT - 1))
                last.then_inc(s_o, 1)

            def turn_attention(t):
                pe.wait_ge(s_on, t + 1)
                nc.tensor.transpose(OB[:, TA:TA + P], on[:, t % 2], idn[:]).then_inc(s_ontps, 1)

            def project(t):
                c = slice((t % TPB) * P, (t % TPB + 1) * P)
                if t == 0:
                    pe.wait_ge(s_ql, B)
                else:
                    pe.wait_ge(s_x2n, t)
                pe.wait_ge(s_ont, t + 1)
                mm(MB[:, 0:P], xc[:, t // TPB, c], idn[:], start=True, stop=False)
                mm(MB[:, 0:P], onT[:, t % 2], w[:, W_O], start=False, stop=True).then_inc(s_rps, 1)

            scores(0)
            for t in range(SLOTS):
                attend = 1 <= t <= NT
                after = 2 <= t < NT + 2
                if t == 0:
                    w2_part(0)
                if after:
                    turn_attention(t - 2)
                if attend:
                    turn_probs(t - 1, 0)
                if after:
                    project(t - 2)
                if attend:
                    turn_probs(t - 1, 1)
                    weigh_values(t - 1, 0)
                    weigh_values(t - 1, 1)
                if t + 1 < NT:
                    scores(t + 1)
                    w2_part(t + 1)

            def ffn_turn(b):
                if b == 0:
                    pe.wait_ge(s_w2, FT)
                if b >= 1:
                    pe.wait_ge(s_x2t, b)
                pe.wait_ge(s_x2n, TPB * (b + 1))
                for i in range(TPB):
                    last = nc.tensor.transpose(FB[:, i * P:(i + 1) * P], x2n[:, b * TPB + i], idn[:])
                last.then_inc(s_x2tps, 1)

            def ffn_hidden(b, j):
                if j == 0:
                    pe.wait_ge(s_x2t, b + 1)
                if b == 0:
                    pe.wait_ge(s_pt, 2 * NT)
                    pe.wait_ge(s_z, NT)
                else:
                    pe.wait_ge(s_h, FT * (b - 1) + j + 1)
                mm(bank[j], w1[:, j * P:(j + 1) * P], x2T[:, b % 2], start=True, stop=True).then_inc(s_hps, 1)

            def ffn_out(b):
                o = bank[4 + b % 2]
                if b < 2:
                    pe.wait_ge(s_on, NT)
                    pe.wait_ge(s_ont, NT)
                else:
                    pe.wait_ge(s_r3, b - 1)
                pe.wait_ge(s_h, FT * (b + 1))
                for i in range(TPB):
                    for j in range(FT):
                        last = mm(o[:, i * P:(i + 1) * P], hT[:, b % 2, j, i * P:(i + 1) * P], w2[:, j],
                                  start=(j == 0), stop=(j == FT - 1))
                last.then_inc(s_fps, 1)

            ffn_turn(0)
            for j in range(FT):
                ffn_hidden(0, j)
            for b in range(B):
                if b + 1 < B:
                    ffn_turn(b + 1)
                    for j in range(FT):
                        ffn_hidden(b + 1, j)
                ffn_out(b)

        @block.scalar
        def _(act):
            def col(c):
                return vec[:, c:c + 1]

            fn = nc.scalar.activation
            act.wait_ge(s_abs, 1)
            fn(spt[:, 1:2], spt[:, 0:1], ACT.Exp, scale=-1.0).then_inc(s_sp_e, 1)
            act.wait_ge(s_lmax, 1)
            for i in range(2):
                last = fn(lg[:, i], lg[:, i], ACT.Exp, bias=lgm[:, i:i + 1], accum_out=lgs[:, i:i + 1])
            last.then_inc(s_lexp, 1)
            act.wait_ge(s_sp_e, 1)
            fn(spt[:, 2:3], spt[:, 1:2], ACT.Ln, bias=1.0).then_inc(s_sp_l, 1)
            act.wait_ge(s_const, 2)
            for b in range(B):
                act.wait_ge(s_x1ps, b + 1)
                fn(x1p[:, b, TW - 1:], bank[b % 2], ACT.Identity, bias=col(V_BX)).then_inc(s_x1, 1)
                act.wait_ge(s_yps, b + 1)
                fn(yy[:, b], bank[2 + b % 2], ACT.Gelu, bias=col(V_BY)).then_inc(s_y, 1)
                act.wait_ge(s_x1, b + 1)
                fn(x2[:, b], x1p[:, b, 0:T], ACT.Identity, scale=col(V_CW), bias=col(V_CB)).then_inc(s_tap0, 1)
            act.wait_ge(s_kps, 1)
            fn(kh[:], bank[4][:, 0:B * M], ACT.Identity, scale=SCALE).then_inc(s_kh, 1)
            for b in range(B):
                act.wait_ge(s_gxps, b + 1)
                fn(gx[:, b], bank[b % 2], ACT.Sigmoid, bias=col(V_GIB)).then_inc(s_gx, 1)
                act.wait_ge(s_gaps, b + 1)
                fn(aa[:, b], bank[2 + b % 2], ACT.Sigmoid, bias=col(V_GAB)).then_inc(s_ga, 1)
            act.wait_ge(s_nsp, 1)
            for b in range(B):
                act.wait_ge(s_ga, b + 1)
                fn(uu[:, b], aa[:, b], ACT.Exp, scale=spt[:, 5:6]).then_inc(s_u, 1)
                fn(aa[:, b], aa[:, b], ACT.Exp, scale=spt[:, 4:5]).then_inc(s_a, 1)
            for b in range(B):
                act.wait_ge(s_u, b + 1)
                fn(uu[:, b], uu[:, b], ACT.Relu, scale=-1.0, bias=1.0).then_inc(s_um, 1)
                act.wait_ge(s_um, b + 1)
                fn(uu[:, b], uu[:, b], ACT.Sqrt).then_inc(s_mult, 1)
            act.wait_ge(s_w1ps, 1)
            nc.scalar.copy(w1[:], FB).then_inc(s_w1, 1)

            def take_w2(j):
                act.wait_ge(s_w2ps, j + 1)
                nc.scalar.copy(w2[:, j], FB[:, 0:D]).then_inc(s_w2, 1)

            def ln1(b):
                act.wait_ge(s_rstd, b + 1)
                if b == KSR0 // (TPB * D):
                    act.wait_ge(s_ks, 1)
                for i in range(TPB):
                    last = fn(x1n[:, b * TPB + i], bank[3 + b % 2][:, i * P:(i + 1) * P], ACT.Identity,
                              scale=rs[:, b % 2, i:i + 1], bias=nb[:, b % 2, i:i + 1])
                last.then_inc(s_x1n, 1)

            def take_ln1(b):
                act.wait_ge(s_x1tps, b + 1)
                nc.scalar.copy(x2[:, b], OB).then_inc(s_x1t, 1)
                fn(xc[:, b], OB, ACT.Identity, bias=col(V_BO)).then_inc(s_x1b, 1)

            def take_q(b):
                act.wait_ge(s_qps, b + 1)
                if b >= 2:
                    act.wait_ge(s_qs[b % 2], 16 * 4 * NG)
                fn(qh[:, b % 2], MB, ACT.Identity, bias=col(V_BQ)).then_inc(s_qh, 1)

            for b in range(B):
                ln1(b)
                take_ln1(b)
                take_q(b)

            def probs(t, f):
                n = 2 * t + f
                act.wait_ge(s_zc, t + 1)
                if n >= 2:
                    act.wait_ge(s_ptps, n - 1)
                fn(pb[:, f, 0:HALF], zb[t % 2][:, f * HALF:(f + 1) * HALF], ACT.Exp).then_inc(s_p, 1)

            def take_probs(t, f):
                n = 2 * t + f
                act.wait_ge(s_ptps, n + 1)
                if n >= 2:
                    act.wait_ge(s_o, n - 1)
                nc.scalar.copy(ptb[:, f], PT).then_inc(s_pt, 1)

            def take_attention(t):
                act.wait_ge(s_ontps, t + 1)
                nc.scalar.copy(onT[:, t % 2], OB[:, TA:TA + P]).then_inc(s_ont, 1)

            def ln2(t):
                act.wait_ge(s_rstd, B + t + 1)
                fn(x2n[:, t], MB[:, 0:P], ACT.Identity, scale=rs[:, t % 2, 0:1],
                   bias=nb[:, t % 2, 0:1]).then_inc(s_x2n, 1)

            for t in range(SLOTS):
                attend = 1 <= t <= NT
                if attend:
                    probs(t - 1, 0)
                    probs(t - 1, 1)
                if 2 <= t < NT + 2:
                    take_attention(t - 2)
                if t >= 3:
                    ln2(t - 3)
                if attend:
                    take_probs(t - 1, 0)
                    take_probs(t - 1, 1)
                if t % 4 == 3 and t < NT:
                    take_w2(t // 4)

            for b in range(B):
                act.wait_ge(s_x2tps, b + 1)
                if b >= 2:
                    act.wait_ge(s_hps, FT * (b - 1))
                nc.scalar.copy(x2T[:, b % 2], FB).then_inc(s_x2t, 1)
                if b >= 2:
                    act.wait_ge(s_fps, b - 1)
                for j in range(FT):
                    act.wait_ge(s_hps, FT * b + j + 1)
                    fn(hT[:, b % 2, j], bank[j], ACT.Gelu_apprx_tanh).then_inc(s_h, 1)

        @block.vector
        def _(dve):
            steps = [0]

            def step(ins):
                steps[0] += 1
                ins.then_inc(s_dve, 1)
                dve.wait_ge(s_dve, steps[0])

            v = nc.vector
            v.memset(mhalf[:], -0.5).then_inc(s_const, 1)
            dve.wait_ge(ld["vec"], 16)
            step(v.tensor_scalar(spt[:, 6:7], vec[:, V_AP:V_AP + 1], -1.0, None, ALU.mult))
            v.tensor_tensor(spt[:, 0:1], spt[:, 6:7], vec[:, V_AP:V_AP + 1], ALU.max).then_inc(s_abs, 1)
            dve.wait_ge(ld["lg"], 16)
            step(v.tensor_reduce(lgm[:], lg[:], AX_X, ALU.max))
            v.tensor_scalar(lgm[:], lgm[:], -1.0, None, ALU.mult).then_inc(s_lmax, 1)
            dve.wait_ge(s_lexp, 1)
            step(v.reciprocal(lgs[:], lgs[:]))
            hp = P // 2
            for i in range(2):
                for q in range(2):
                    last = v.tensor_scalar(wsel[q * hp:(q + 1) * hp, i],
                                           lg[q * hp:(q + 1) * hp, i].rearrange("p (k q) -> p q k", q=2)[:, q],
                                           lgs[q * hp:(q + 1) * hp, i:i + 1], None, ALU.mult)
            last.then_inc(s_wsel, 1)
            dve.wait_ge(s_sp_l, 1)
            step(v.scalar_tensor_tensor(spt[:, 3:4], vec[:, V_AP:V_AP + 1], 0.0, spt[:, 2:3], ALU.max, ALU.add))
            step(v.tensor_scalar(spt[:, 4:5], spt[:, 3:4], -C_GATE, None, ALU.mult))
            v.tensor_scalar(spt[:, 5:6], spt[:, 3:4], -2.0 * C_GATE, None, ALU.mult).then_inc(s_nsp, 1)

            def v_heads(n):
                b, f = divmod(n, 2)
                dve.wait_ge(s_vps, n + 1)
                v.tensor_copy(vhat[:, b, f, :, :, HD:VC], vm[:].unsqueeze(3))
                v.tensor_tensor(vhat[:, b, f, :, :, 0:HD].rearrange("p i h c -> p (i h) c"),
                                bank[5 + n % 2][:, 0:RT * HH * HD].rearrange("p (n c) -> p n c", c=HD),
                                vm[:].rearrange("p i h -> p (i h)").unsqueeze(2).to_broadcast([P, RT * HH, HD]),
                                ALU.mult).then_inc(s_vhat, 1)

            for b in range(B):
                dve.wait_ge(s_tap0, b + 1)
                for i in range(1, TW):
                    ins = v.scalar_tensor_tensor(x2[:, b], x1p[:, b, i:i + T], vec[:, V_CW + i:V_CW + i + 1],
                                                 x2[:, b], ALU.mult, ALU.add)
                    if i < TW - 1:
                        step(ins)
                ins.then_inc(s_x2, 1)
                if b == B - 1:
                    dve.wait_ge(s_kh, 1)
                    v.scalar_tensor_tensor(kl[:], bank[4][:, 0:B * M], SCALE, kh[:].bitcast(F32), ALU.mult,
                                           ALU.subtract).then_inc(s_kl, 1)
                if b == 0:
                    dve.wait_ge(ld["vm"], 16)
                v_heads(2 * b)
                v_heads(2 * b + 1)

            def gate_input(b):
                dve.wait_ge(s_gx, b + 1)
                v.tensor_tensor(gx[:, b], gx[:, b], x2[:, b], ALU.mult).then_inc(s_gin, 1)

            def recur(b):
                dve.wait_ge(s_mult, b + 1)
                dve.wait_ge(s_a, b + 1)
                v.memset(aa[:, b, 0:1], 0.0)
                step(v.memset(uu[:, b, 0:1], 1.0))
                dve.wait_ge(s_gin, b + 1)
                step(v.tensor_tensor(gx[:, b], gx[:, b], uu[:, b], ALU.mult))
                step(v.tensor_tensor_scan(uu[:, b], aa[:, b], gx[:, b], 0.0, ALU.mult, ALU.add))
                dve.wait_ge(s_y, b + 1)
                step(v.tensor_tensor(yy[:, b], yy[:, b], uu[:, b], ALU.mult))
                v.tensor_tensor(xc[:, b], xc[:, b], yy[:, b], ALU.add).then_inc(s_r1, 1)

            def stats(src, slot, n):
                for i in range(n):
                    ins = v.bn_stats(st[:, slot, i], src(i))
                step(ins)
                for i in range(n):
                    ins = v.bn_aggr(mv[:, slot, i], st[:, slot, i])
                ins.then_inc(s_var, 1)

            def ln1_stats(b):
                dve.wait_ge(s_r1ps, b + 1)
                if b >= 2:
                    dve.wait_ge(s_x1n, b - 1)
                stats(lambda i: bank[3 + b % 2][:, i * P:(i + 1) * P], b % 2, TPB)

            def q_low(b):
                dve.wait_ge(s_qh, b + 1)
                if b >= 2:
                    dve.wait_ge(s_qs[b % 2], 16 * 4 * NG)
                v.scalar_tensor_tensor(ql[:, b % 2], MB, vec[:, V_BQ:V_BQ + 1], qh[:, b % 2].bitcast(F32), ALU.add,
                                       ALU.subtract).then_inc(s_ql, 1)

            for b in range(B):
                gate_input(b)
            recur(0)
            recur(1)
            ln1_stats(0)
            recur(2)
            ln1_stats(1)
            q_low(0)
            recur(3)
            ln1_stats(2)
            q_low(1)
            ln1_stats(3)
            q_low(2)
            q_low(3)

            def shift_scores(t, between):
                dve.wait_ge(s_sps, t + 1)
                sc = SC.rearrange("p (h m) -> p h m", m=M)
                step(v.tensor_reduce(mx[:], sc, AX_X, ALU.max))
                step(v.tensor_scalar(mc[:], mx[:], CLAMP, -CLAMP, ALU.min, ALU.max))
                if t >= 2:
                    dve.wait_ge(s_p, 2 * (t - 1))
                v.scalar_tensor_tensor(zb[t % 2].rearrange("p (h m) -> p h m", m=M), sc, -CLAMP,
                                       mc[:].unsqueeze(2).to_broadcast([P, H, M]),
                                       ALU.max, ALU.subtract).then_inc(s_z, 1)
                between()
                dve.wait_ge(s_z, t + 1)
                v.tensor_scalar(zb[t % 2], zb[t % 2], 0.0, None, ALU.min).then_inc(s_zc, 1)

            def norm_heads(t):
                dve.wait_ge(s_o, 2 * (t + 1))
                if t >= 2:
                    dve.wait_ge(s_ontps, t - 1)
                o = OB[:, 0:H * VC].rearrange("p (h c) -> p h c", c=VC)
                step(v.reciprocal(rden[:, t % 2], o[:, :, HD]))
                v.tensor_tensor(on[:, t % 2].rearrange("p (h c) -> p h c", c=HD), o[:, :, 0:HD],
                                rden[:, t % 2].unsqueeze(2).to_broadcast([P, H, HD]), ALU.mult).then_inc(s_on, 1)

            def ln2_stats(t):
                dve.wait_ge(s_rps, t + 1)
                if t < 2:
                    dve.wait_ge(s_x1n, B)
                v.bn_stats(st[:, t % 2, 0], MB[:, 0:P]).then_inc(s_st2, 1)

            def ln2_mean(t):
                dve.wait_ge(s_st2, t + 1)
                if t >= 2:
                    dve.wait_ge(s_rstd, B + t - 1)
                v.bn_aggr(mv[:, t % 2, 0], st[:, t % 2, 0]).then_inc(s_var, 1)

            for t in range(SLOTS):
                after = 2 <= t < NT + 2
                if after:
                    norm_heads(t - 2)

                def between():
                    if after:
                        ln2_stats(t - 2)

                if t < NT:
                    shift_scores(t, between)
                else:
                    between()
                if after:
                    ln2_mean(t - 2)

            for b in range(B):
                dve.wait_ge(s_fps, b + 1)
                if b >= 1:
                    dve.wait_ge(s_out, b)
                v.tensor_tensor(rr.rearrange("p t d -> p (t d)"), bank[4 + b % 2],
                                x2n[:, b * TPB:(b + 1) * TPB].rearrange("p t d -> p (t d)"),
                                ALU.add).then_inc(s_r3, 1)
                dve.wait_ge(s_r3, b + 1)
                for i in range(TPB):
                    ins = v.bn_stats(st3[:, i], rr[:, i])
                step(ins)
                for i in range(TPB):
                    ins = v.bn_aggr(mv3[:, i], st3[:, i])
                ins.then_inc(s_var3, 1)
                dve.wait_ge(s_rstd3, b + 1)
                if b >= 2:
                    dve.wait_ge(s_st[b - 2], 16)
                for i in range(TPB):
                    ins = v.tensor_scalar(ot[:, b % 2, i], rr[:, i], mv3[:, i, 0:1], rs3[:, i:i + 1],
                                          ALU.subtract, ALU.mult)
                ins.then_inc(s_out, 1)

        @block.gpsimd
        def _(pool):
            g = nc.gpsimd
            g.memset(x1p[:, :, 0:TW - 1], 0.0).then_inc(s_const, 1)
            pool.wait_ge(s_wsel, 1)
            pool.wait_ge(ld["a1"], 16)
            g.tensor_tensor(a1[:], a1[:], wsel[:, 0, :].unsqueeze(2).to_broadcast([P, KT, D]),
                            ALU.mult).then_inc(s_a1w, 1)
            pool.wait_ge(s_kst, 16 * 4 * NG)
            pool.wait_ge(ld["hm"], 16)
            for b in range(B):
                for gr in range(NG):
                    last = g.tensor_tensor(ks[:, b, gr].rearrange("p (h m) -> p h m", m=M),
                                           ksr[:, gr, b * M:(b + 1) * M].unsqueeze(1).to_broadcast([P, 4, M]),
                                           hm[:].unsqueeze(2).to_broadcast([P, 4, M]), ALU.mult)
            last.then_inc(s_ks, 1)
            pool.wait_ge(ld["b2"], 16)
            g.tensor_tensor(b2s[:], b2s[:], wsel[:, 1, :].unsqueeze(2).to_broadcast([P, KT, D]),
                            ALU.mult).then_inc(s_b2w, 1)

            steps = [0]

            def step(ins):
                steps[0] += 1
                ins.then_inc(s_pool, 1)
                pool.wait_ge(s_pool, steps[0])

            def root(n, slot, width):
                pool.wait_ge(s_var, n + 1)
                step(g.tensor_scalar(ve[:, slot, 0:width], mv[:, slot, 0:width, 1], EPS, 1.0, ALU.add, ALU.mult))
                step(g.tensor_tensor(rs[:, slot, 0:width], ve[:, slot, 0:width], mhalf[:, 0:width], ALU.pow))
                step(g.tensor_tensor(ve[:, slot, 0:width], mv[:, slot, 0:width, 0], rs[:, slot, 0:width], ALU.mult))
                g.tensor_scalar(nb[:, slot, 0:width], ve[:, slot, 0:width], 0.0, -1.0, ALU.add,
                                ALU.mult).then_inc(s_rstd, 1)

            def root3(b):
                pool.wait_ge(s_var3, b + 1)
                step(g.tensor_scalar(ve3[:], mv3[:, :, 1], EPS, 1.0, ALU.add, ALU.mult))
                g.tensor_tensor(rs3[:], ve3[:], mhalf[:], ALU.pow).then_inc(s_rstd3, 1)

            pool.wait_ge(s_w1ps, 1)
            g.memset(pb[:, :, HALF:PADW], 0.0).then_inc(s_pad, 1)
            pool.wait_ge(s_const, 2)
            for b in range(B):
                root(b, b % 2, TPB)
            for t in range(NT):
                root(B + t, t % 2, 1)
            for b in range(B):
                root3(b)


def kernel(x, ctx_768, L0_attn_w_x, L0_attn_b_x, L0_attn_w_y, L0_attn_b_y, L0_attn_conv_w, L0_attn_conv_b,
           L0_attn_gi_w, L0_attn_gi_b, L0_attn_ga_w, L0_attn_ga_b, L0_attn_a_param, L0_xattn_Wq, L0_xattn_bq,
           L0_xattn_Wk, L0_xattn_bk, L0_xattn_Wv, L0_xattn_bv, L0_xattn_Wo, L0_xattn_bo, L0_ffn_fc1_A,
           L0_ffn_fc1_B, L0_ffn_fc2_A, L0_ffn_fc2_B, L0_ffn_fc1_logits, L0_ffn_fc2_logits):
    import concourse.bacc as bacc
    from concourse.bass_utils import run_bass_kernel_spmd

    c = np.ascontiguousarray
    a = {}
    a["xT"] = c(np.transpose(x, (2, 0, 1)))
    a["vecs"] = c(np.stack([*L0_attn_conv_w, L0_attn_b_x, L0_attn_b_y, L0_attn_conv_b, L0_attn_gi_b,
                            L0_attn_ga_b, L0_attn_a_param, L0_xattn_bq, L0_xattn_bo], axis=1))
    a["wpack"] = c(np.stack([L0_attn_w_x, L0_attn_w_y, L0_attn_gi_w, L0_attn_ga_w, L0_xattn_Wq, L0_xattn_Wo],
                            axis=1))
    ctxT = np.transpose(ctx_768, (2, 0, 1))
    ctxT = np.concatenate([ctxT, ctxT, ctxT], axis=2).reshape(DC, B * 3 * M)
    ctxT = np.concatenate([ctxT, np.ones((1, B * 3 * M), np.float32)], axis=0)
    wkv = np.concatenate([np.concatenate([L0_xattn_Wk, L0_xattn_bk[None]], axis=0),
                          np.concatenate([L0_xattn_Wv, L0_xattn_bv[None]], axis=0)], axis=1)
    a["kvpack"] = c(np.concatenate([ctxT, wkv], axis=1))
    a["logits"] = c(np.stack([L0_ffn_fc1_logits, L0_ffn_fc2_logits]))
    a["a1T"] = c(np.transpose(np.transpose(L0_ffn_fc1_A, (0, 2, 1)).reshape(KT, P, D), (1, 0, 2)))
    a["b1"] = c(np.transpose(L0_ffn_fc1_B.reshape(KT, P, F), (1, 0, 2)))
    a["a2T"] = c(np.transpose(np.transpose(L0_ffn_fc2_A, (0, 2, 1)).reshape(KT, P, F), (1, 0, 2)))
    a["b2"] = c(np.transpose(L0_ffn_fc2_B.reshape(KT, P, D), (1, 0, 2)))
    a["ident"] = np.eye(P, dtype=np.float32)
    a["hmask"] = c(np.tile(np.repeat(np.eye(4, dtype=np.float32), HD, axis=0), (4, 1)))
    row = np.arange(PADW)
    a["vmask"] = c(np.transpose((row[:, None] // M == np.arange(HH)[None]).astype(np.float32).reshape(RT, P, HH),
                                (1, 0, 2)))
    nc = bacc.Bacc("TRN2", target_bir_lowering=False, num_devices=1)
    names = ["xT", "vecs", "wpack", "kvpack", "logits", "a1T", "b1", "a2T", "b2", "ident", "hmask", "vmask"]
    arrays = {f"in_{n}": a[n] for n in names}
    args = [nc.dram_tensor(f"in_{n}", a[n].shape, F32, kind="ExternalInput").ap() for n in names]
    out = nc.dram_tensor("out", (B, T, D), F32, kind="ExternalOutput").ap()
    build(nc, *args, out)
    r = run_bass_kernel_spmd(nc, [arrays], core_ids=[0])
    return r.results[0]["out"]
```

```python
from contextlib import ExitStack

import numpy as np

import concourse.bass as bass
from concourse import mybir

ALU = mybir.AluOpType
ACT = mybir.ActivationFunctionType
F32 = mybir.dt.float32
F32R = mybir.dt.float32r
AX_X = mybir.AxisListType.X

P = 128
B, T, D = 4, 512, 128
TPB = T // P
NT = B * TPB
M, DC = 77, 96
H = 16
HD = D // H
HH = H // 2
HALF = HH * M
NG = H // 4
QUAD = 4 * M
RT = -(-HALF // P)
PADW = RT * P
VC = HD + 1
NP_, R, F = 32, 64, 512
KT = NP_ * R // P
FT = F // P
UT = TPB // 2
NU = NT // UT
OT_N = 4
TW = 4
C_GATE = 8.0
CLAMP = 10000.0
SCALE = float(HD) ** -0.5
EPS = 1e-5

V_CW, V_BX, V_BY, V_CB, V_GIB, V_GAB, V_AP, V_BQ, V_BQS = 0, 4, 5, 6, 7, 8, 9, 10, 11
V_N = V_BQS + NG
W_X, W_Y, W_GI, W_GA, W_Q, W_O, W_QS = range(7)
W_N = W_QS + NG
VR_ENDS = sorted({*range(0, PADW, M), *range(0, PADW + 1, P)})
VR_CUTS = list(zip(VR_ENDS[:-1], VR_ENDS[1:]))


def build(nc, xT, vecs, wpack, kvpack, logits, a1T, b1, a2T, b2, ident, hmask, vmask, bo, out):
    with ExitStack() as ctx:
        def sb(name, shape, dt=F32):
            return ctx.enter_context(nc.sbuf_tensor(name, shape, dt))

        def sem(name):
            return ctx.enter_context(nc.semaphore(name))

        xc = sb("xc", [P, B, T])
        x1p = sb("x1p", [P, B, T + TW - 1])
        x2 = sb("x2", [P, B, T])
        gx = sb("gx", [P, B, T])
        aa = sb("aa", [P, B, T])
        uu = sb("uu", [P, B, T])
        yy = sb("yy", [P, B, T])
        x1n = x1p[:].rearrange("p b t -> p (b t)")[:, 0:NT * D].rearrange("p (n d) -> p n d", d=D)
        x2n = aa[:].rearrange("p b (t d) -> p (b t) d", d=D)
        x2T = yy
        vec = sb("vec", [P, V_N])
        w = sb("w", [P, W_N, D])
        bor = sb("bor", [P, D])
        r2 = sb("r2", [P, 2, D])
        kvp = sb("kvp", [DC + 1, B * M + (NG + 1) * D])
        idn = sb("idn", [P, P])
        hm = sb("hm", [P, 4])
        vm = sb("vm", [P, RT, HH])
        lg = sb("lg", [P, 2, NP_])
        lgm = sb("lgm", [P, 2])
        lgs = sb("lgs", [P, 2])
        wsel = sb("wsel", [P, 2, KT])
        spt = sb("spt", [P, 8])
        a1 = sb("a1", [P, KT, D])
        b1s = sb("b1s", [P, KT, F])
        a2 = sb("a2", [P, KT, F])
        b2s = sb("b2s", [P, KT, D])
        w1 = sb("w1", [P, F])
        w2 = sb("w2", [P, FT, D])
        qh, ql = gx[:].bitcast(F32R), uu[:].bitcast(F32R)
        qs = sb("qs", [P, 2, NG, T], F32R)
        ks = sb("ks", [P, B, NG, QUAD], F32R)
        kst = sb("kst", [P, NG, B * M], F32R)
        vt = sb("vt", [M, B * D])
        vr = b1s[:, 0:RT]
        vhat = sb("vhat", [P, B, 2, RT, HH, VC])
        z2 = a1[:].rearrange("p k d -> p (k d)")
        late = b1s[:, KT // 2:].rearrange("p k f -> p (k f)")
        zb = [late[:, 0:H * M], z2[:, 0:H * M]]
        pb = late[:, H * M:H * M + 2 * PADW].rearrange("p (f c) -> p f c", f=2)
        ptb = late[:, H * M + 2 * PADW:H * M + 4 * PADW].rearrange("p (f c) -> p f c", f=2)
        oT = late[0:HH * VC, H * M + 4 * PADW:H * M + 4 * PADW + 2 * P]
        mx = sb("mx", [P, H])
        mc = sb("mc", [P, H])
        rden = sb("rden", [P, 2, H])
        st = sb("st", [P, 2, TPB, 6])
        mv = sb("mv", [P, 2, TPB, 2])
        ve = sb("ve", [P, 2, TPB])
        rs = sb("rs", [P, 2, TPB])
        nb = sb("nb", [P, 2, TPB])
        st3 = sb("st3", [P, 2, UT, 6])
        mv3 = sb("mv3", [P, 2, UT, 2])
        ve3 = sb("ve3", [P, 2, UT])
        rs3 = sb("rs3", [P, 2, UT])
        mhalf = sb("mhalf", [P, TPB])
        ot = a1[:, 0:OT_N * UT].rearrange("p (s t) d -> p s t d", t=UT)
        rr = a1[:, OT_N * UT:(OT_N + 2) * UT].rearrange("p (s t) d -> p s t d", t=UT)
        on = a1[:, 3 * TPB:3 * TPB + 2]
        onT = a1[:, 3 * TPB + 2:4 * TPB]
        hT = b1s[:, 0:2 * FT].rearrange("p (s f) t -> p s f t", f=FT)

        ps = ctx.enter_context(nc.psum_tensor("ps", [P, 8, 512], F32))
        bank = [ps[:, i, :] for i in range(8)]
        flat = ps[:].rearrange("p a c -> p (a c)")
        SC = flat[:, 0:H * M]
        PT = flat[:, 3 * 512:3 * 512 + PADW]
        OB, MB, FB = bank[5], bank[6], bank[7]
        HC = HH * VC
        KPS = ps[:, 4:4 + NG - 1, :]
        AT, AN, TA = OB[0:HC, 0:2 * P], FB[:, 0:H * VC], FB[:, 256:256 + P]
        TX = FB[:, 256 + P:]

        ld = {n: sem(f"ld_{n}") for n in ("vec", "x0", "x1", "x2", "x3", "w", "w2", "kv", "lg", "a1",
                                          "b1a", "b1b", "b2", "a2a", "a2b", "id", "hm", "vm", "bo")}
        s_const = sem("const_ready")
        s_abs = sem("abs_a_param")
        s_sp_e = sem("softplus_exp")
        s_sp_l = sem("softplus_ln")
        s_nsp = sem("neg_softplus_ready")
        s_lmax = sem("logit_max")
        s_lexp = sem("logit_exp")
        s_wsel = sem("primitive_weights")
        s_a1w = sem("a1_weighted")
        s_b2w = sem("b2_weighted")
        s_x1ps = sem("x1_in_psum")
        s_yps = sem("y_in_psum")
        s_x1 = sem("x1_ready")
        s_tap0 = sem("first_tap_ready")
        s_x2 = sem("conv_ready")
        s_gxps = sem("gate_x_in_psum")
        s_gaps = sem("gate_a_in_psum")
        s_gx = sem("gate_x_ready")
        s_ga = sem("gate_a_ready")
        s_y = sem("gelu_ready")
        s_u = sem("a_squared_ready")
        s_uc = sem("a_squared_capped")
        s_a = sem("a_ready")
        s_mult = sem("multiplier_ready")
        s_hy = sem("hy_ready")
        s_r1 = sem("r1_ready")
        s_r1ps = sem("r1_turned")
        s_x1n = sem("ln1_ready")
        s_x1tps = sem("ln1_turned")
        s_x1t = sem("ln1_channel_major")
        s_x1b = sem("ln1_with_bo")
        s_r2 = sem("r2_ready")
        s_qps = sem("q_in_psum")
        s_q0ps = sem("q0_stack_in_psum")
        s_q0h = sem("q0_stack_high")
        s_q0l = sem("q0_stack_low")
        s_qh = sem("q_high_ready")
        s_ql = sem("q_low_ready")
        s_qs = [sem(f"q_stacked_{i}") for i in range(2)]
        s_kps = sem("k_in_psum")
        s_kh = sem("k_high_ready")
        s_kl = sem("k_low_ready")
        s_ks = sem("k_heads_apart")
        s_vps = sem("v_in_psum")
        s_vt = sem("v_ready")
        s_vr = sem("v_rows_in_order")
        s_vhat = sem("vhat_ready")
        s_ones = sem("vhat_ones_ready")
        s_w1ps = sem("w1_in_psum")
        s_w1 = sem("w1_ready")
        s_w2ps = sem("w2_in_psum")
        s_w2 = sem("w2_ready")
        s_sps = sem("scores_in_psum")
        s_top = sem("top_scores")
        s_ctop = sem("top_scores_clipped")
        s_z = sem("shifted_scores")
        s_zc = sem("capped_scores")
        s_zn = sem("capped_scores_negated")
        s_p = sem("probs_ready")
        s_ptps = sem("probs_turned")
        s_pt = sem("turned_probs_ready")
        s_ot = sem("attention_channel_major")
        s_ots = sem("attention_in_sbuf")
        s_o = sem("attention_token_major")
        s_rden = sem("sums_inverted")
        s_on = sem("attention_normed")
        s_ontps = sem("attention_turned")
        s_ont = sem("turned_attention_ready")
        s_rps = sem("projection_in_psum")
        s_var = sem("variance_ready")
        s_rstd = sem("rstd_ready")
        s_x2n = sem("ln2_ready")
        s_x2tps = sem("ln2_turned")
        s_x2t = sem("ln2_channel_major")
        s_hps = sem("hidden_in_psum")
        s_h = sem("hidden_ready")
        s_fps = sem("ffn_in_psum")
        s_r3 = sem("r3_ready")
        s_out = sem("output_ready")
        s_st = [sem(f"output_stored_{i}") for i in range(OT_N)]
        s_var3 = sem("variance3_ready")
        s_rstd3 = sem("rstd3_ready")
        s_gin = sem("gated_input")
        s_pad = sem("probs_padding_zeroed")
        s_st2 = sem("ln2_statistics")
        s_dve = sem("vector_step")
        s_pool = sem("pool_step")

        block = ctx.enter_context(nc.Block())

        Q0_BANKS = (0, 1, 2, 6)
        W2_LATE = (FT - 1) * KT
        Y_BANKS = (2, 3, 7, 1)

        @block.sync
        def _(sp):
            sp.dma_start(xc[:, 0], xT[:, 0]).then_inc(ld["x0"], 16)
            sp.dma_start(w[:, 0:2], wpack[:, 0:2]).then_inc(ld["w"], 16)
            sp.dma_start(vec[:], vecs).then_inc(ld["vec"], 16)
            sp.dma_start(lg[:], logits.partition_broadcast(P)).then_inc(ld["lg"], 16)
            for b in range(1, B):
                sp.dma_start(xc[:, b], xT[:, b]).then_inc(ld[f"x{b}"], 16)
            sp.dma_start(kvp[:], kvpack).then_inc(ld["kv"], 16)
            sp.dma_start(w[:, 2:], wpack[:, 2:]).then_inc(ld["w2"], 16)
            sp.dma_start(vm[:], vmask).then_inc(ld["vm"], 16)
            sp.dma_start(a1[:], a1T).then_inc(ld["a1"], 16)
            sp.dma_start(hm[:], hmask).then_inc(ld["hm"], 16)
            sp.dma_start(b1s[:, 0:KT // 2], b1[:, 0:KT // 2]).then_inc(ld["b1a"], 16)
            sp.dma_start(b2s[:], b2).then_inc(ld["b2"], 16)
            sp.dma_start(idn[:], ident).then_inc(ld["id"], 16)
            sp.dma_start(bor[:], bo.partition_broadcast(P)).then_inc(ld["bo"], 16)
            sp.dma_start(b1s[:, KT // 2:], b1[:, KT // 2:]).then_inc(ld["b1b"], 16)
            sp.dma_start(a2[:, 0:KT // 2], a2T[:, 0:KT // 2]).then_inc(ld["a2a"], 16)
            sp.dma_start(a2[:, KT // 2:], a2T[:, KT // 2:]).then_inc(ld["a2b"], 16)
            sp.wait_ge(s_vt, 1)
            sp.wait_ge(s_w1ps, 1)
            for lo, hi in VR_CUTS:
                i, at = divmod(lo, P)
                sp.dma_start(vr[at:at + hi - lo, i], vt[lo % M:lo % M + hi - lo]).then_inc(s_vr, 16)
            for b in range(1, B):
                sp.wait_ge(s_qh, b)
                sp.wait_ge(s_ql, b)
                if b >= 2:
                    sp.wait_ge(s_sps, TPB * (b - 1))
                for i, part in enumerate((qh, qh, ql, ql)):
                    for g in range(NG):
                        sp.dma_start(qs[32 * i:32 * i + 32, b % 2, g].bitcast(F32),
                                     part[32 * g:32 * g + 32, b].bitcast(F32)).then_inc(s_qs[b % 2], 16)
            for u in range(NU):
                b, i = divmod(u * UT, TPB)
                sp.wait_ge(s_out, u + 1)
                sp.dma_start(out[b, i * P:(i + UT) * P].rearrange("(t p) d -> p t d", p=P),
                             ot[:, u % OT_N]).then_inc(s_st[u % OT_N], 16)
            for i in range(OT_N):
                sp.wait_ge(s_st[i], 16 * (NU // OT_N))

        @block.tensor
        def _(pe):
            mm = nc.tensor.matmul
            def branch_x(b):
                pe.wait_ge(ld[f"x{b}"], 16)
                if b >= 2:
                    pe.wait_ge(s_x1, b - 1)
                mm(bank[b % 2], w[:, W_X], xc[:, b], start=True, stop=True).then_inc(s_x1ps, 1)

            def branch_y(b):
                if b == 3:
                    pe.wait_ge(s_x1, 4)
                mm(bank[Y_BANKS[b]], w[:, W_Y], xc[:, b], start=True, stop=True).then_inc(s_yps, 1)

            pe.wait_ge(ld["w"], 16)
            for b in range(2):
                branch_x(b)
                branch_y(b)
            branch_x(2)
            branch_x(3)
            pe.wait_ge(ld["kv"], 16)
            ctxT = kvp[:, 0:B * M]
            wv = kvp[:, B * M + NG * D:]
            for g in range(NG):
                wk = kvp[:, B * M + g * D:B * M + (g + 1) * D]
                if g < NG - 1:
                    mm(KPS[:, g, 0:B * M], wk, ctxT, start=True, stop=True)
                else:
                    for i in range(2):
                        last = mm(KPS[:, i, B * M:B * M + 2 * M], wk, ctxT[:, 2 * i * M:2 * (i + 1) * M],
                                  start=True, stop=True)
            last.then_inc(s_kps, 1)
            branch_y(2)
            branch_y(3)

            def gates(b):
                pe.wait_ge(s_x2, b + 1)
                if b == 0:
                    pe.wait_ge(ld["w2"], 16)
                    pe.wait_ge(s_x1, B)
                if b == 1:
                    pe.wait_ge(s_y, B)
                if b >= 2:
                    pe.wait_ge(s_gx, b - 1)
                mm(bank[b % 2], w[:, W_GI], x2[:, b], start=True, stop=True).then_inc(s_gxps, 1)
                if b == 0:
                    pe.wait_ge(s_y, 2)
                if b >= 2:
                    pe.wait_ge(s_ga, b - 1)
                mm(bank[2 + b % 2], w[:, W_GA], x2[:, b], start=True, stop=True).then_inc(s_gaps, 1)

            def values():
                pe.wait_ge(s_kl, 1)
                for b in range(B):
                    last = mm(bank[5][0:M, b * D:(b + 1) * D], ctxT[:, b * M:(b + 1) * M], wv, start=True, stop=True)
                last.then_inc(s_vps, 1)

            def compose_w1(lo, hi):
                for k in range(lo, hi):
                    if k == 0:
                        pe.wait_ge(s_a1w, 1)
                        pe.wait_ge(s_kl, 1)
                    if k % (KT // 2) == 0:
                        pe.wait_ge(ld["b1a" if k == 0 else "b1b"], 16)
                    last = mm(MB, a1[:, k], b1s[:, k], start=(k == 0), stop=(k == KT - 1))
                    if k == KT - 1:
                        last.then_inc(s_w1ps, 1)

            def compose_w2(lo, hi):
                for n in range(lo, hi):
                    j, k = divmod(n, KT)
                    if n == 0:
                        pe.wait_ge(s_y, B)
                        pe.wait_ge(s_b2w, 1)
                    if n == W2_LATE:
                        pe.wait_ge(s_z, NT)
                    if j == 0 and k % (KT // 2) == 0:
                        pe.wait_ge(ld["a2a" if k == 0 else "a2b"], 16)
                    o = FB[:, j * D:(j + 1) * D] if n < W2_LATE else bank[2][:, 0:D]
                    last = mm(o, a2[:, k, j * P:(j + 1) * P], b2s[:, k],
                              start=(k == 0), stop=(k == KT - 1))
                    if n + 1 in (W2_LATE, FT * KT):
                        last.then_inc(s_w2ps, 1)

            def turn_r1(b):
                pe.wait_ge(s_r1, b + 1)
                if b == 0:
                    pe.wait_ge(ld["id"], 16)
                    pe.wait_ge(s_ga, B)
                if b >= 2:
                    pe.wait_ge(s_x1n, b - 1)
                for i in range(TPB):
                    last = nc.tensor.transpose(bank[3 + b % 2][:, i * P:(i + 1) * P],
                                               xc[:, b, i * P:(i + 1) * P], idn[:])
                last.then_inc(s_r1ps, 1)

            def turn_ln1(b):
                pe.wait_ge(s_x1n, b + 1)
                if b == 0:
                    pe.wait_ge(s_vt, 1)
                if b >= 1:
                    pe.wait_ge(s_x1t, b)
                for i in range(TPB):
                    last = nc.tensor.transpose(OB[:, i * P:(i + 1) * P], x1n[:, b * TPB + i], idn[:])
                last.then_inc(s_x1tps, 1)

            def stack_q0():
                pe.wait_ge(s_x1t, 1)
                pe.wait_ge(s_w1, 1)
                pe.wait_ge(s_gx, B)
                pe.wait_ge(s_ga, B)
                for g in range(NG):
                    mm(bank[Q0_BANKS[g]], w[:, W_QS + g], x2[:, 0], start=True, stop=True).then_inc(s_q0ps, 1)

            def project_q(b):
                pe.wait_ge(s_x1t, b + 1)
                if b == 1:
                    pe.wait_ge(s_q0l, NG)
                else:
                    pe.wait_ge(s_ql, b - 1)
                mm(MB, w[:, W_Q], x2[:, b], start=True, stop=True).then_inc(s_qps, 1)

            def scores(t):
                b = t // TPB
                if t == 0:
                    pe.wait_ge(s_q0h, NG)
                    pe.wait_ge(s_q0l, NG)
                elif t % TPB == 0:
                    pe.wait_ge(s_qs[b % 2], 16 * 4 * NG * (2 if b == 3 else 1))
                if t % TPB == 0:
                    pe.wait_ge(s_ks, b + 1)
                if t >= 1:
                    pe.wait_ge(s_z, t)
                for g in range(NG):
                    lo = g * QUAD
                    while lo < (g + 1) * QUAD:
                        hi = min((g + 1) * QUAD, (lo // 512 + 1) * 512)
                        last = mm(SC[:, lo:hi], qs[:, b % 2, g, (t % TPB) * P:(t % TPB + 1) * P],
                                  ks[:, b, g, lo - g * QUAD:hi - g * QUAD], start=True, stop=True)
                        lo = hi
                last.then_inc(s_sps, 1)

            def turn_probs(t, f):
                n = 2 * t + f
                pe.wait_ge(s_p, n + 1)
                if n == 0:
                    pe.wait_ge(s_x1n, B)
                    pe.wait_ge(s_pad, 1)
                else:
                    pe.wait_ge(s_pt, n)
                for i in range(RT):
                    last = nc.tensor.transpose(PT[:, i * P:(i + 1) * P], pb[:, f, i * P:(i + 1) * P], idn[:])
                last.then_inc(s_ptps, 1)

            def weigh_values(t, f):
                pe.wait_ge(s_pt, 2 * t + f + 1)
                if t == 0 and f == 0:
                    pe.wait_ge(s_x1t, B)
                    pe.wait_ge(s_ones, 1)
                if t % TPB == 0 and f == 0:
                    pe.wait_ge(s_vhat, t // TPB + 1)
                if t >= 1 and f == 0:
                    pe.wait_ge(s_ots, t)
                for i in range(RT):
                    last = mm(AT[:, f * P:(f + 1) * P], vhat[:, t // TPB, f, i].rearrange("p h c -> p (h c)"),
                              ptb[:, f, i * P:(i + 1) * P], start=(i == 0), stop=(i == RT - 1))
                last.then_inc(s_ot, 1)

            def turn_back(t):
                if t == 0:
                    pe.wait_ge(s_w2, 1)
                else:
                    pe.wait_ge(s_ont, t)
                if t >= 3:
                    pe.wait_ge(s_x2t, t - 2)
                pe.wait_ge(s_ots, t + 1)
                for f in range(2):
                    last = nc.tensor.transpose(AN[:, f * HC:(f + 1) * HC], oT[:, f * P:(f + 1) * P], idn[0:HC, 0:HC])
                last.then_inc(s_o, 1)

            def turn_attention(t):
                pe.wait_ge(s_on, t + 1)
                nc.tensor.transpose(TA, on[:, t % 2], idn[:]).then_inc(s_ontps, 1)

            def turn_ln2(t):
                pe.wait_ge(s_x2n, t + 1)
                if t >= 1:
                    pe.wait_ge(s_x2t, t)
                nc.tensor.transpose(TX, x2n[:, t], idn[:]).then_inc(s_x2tps, 1)

            def project(t):
                pe.wait_ge(s_ont, t + 1)
                if t == 0:
                    pe.wait_ge(s_ql, B - 1)
                else:
                    pe.wait_ge(s_r2, t)
                mm(MB[:, 0:P], onT[:, t % 2], w[:, W_O], start=True, stop=True).then_inc(s_rps, 1)

            for b in range(B):
                gates(b)
            values()
            compose_w1(0, 12)
            turn_r1(0)
            compose_w1(12, 14)
            turn_r1(1)
            compose_w1(14, 16)
            compose_w2(0, 11)
            turn_ln1(0)
            compose_w2(11, 13)
            stack_q0()
            compose_w2(13, 15)
            turn_r1(2)
            compose_w2(15, 19)
            scores(0)
            compose_w2(19, 21)
            turn_r1(3)
            turn_ln1(1)
            compose_w2(21, 30)
            project_q(1)
            compose_w2(30, 35)
            scores(1)
            turn_ln1(2)
            compose_w2(35, 39)
            project_q(2)
            compose_w2(39, 43)
            turn_ln1(3)
            compose_w2(43, 45)
            turn_probs(0, 0)
            project_q(3)
            compose_w2(45, W2_LATE)
            for t in range(NT):
                if t + 2 < NT:
                    scores(t + 2)
                turn_probs(t, 1)
                if t == NT - 2:
                    compose_w2(W2_LATE, 50)
                if t >= 1:
                    turn_back(t - 1)
                weigh_values(t, 0)
                if t == NT - 2:
                    compose_w2(50, 52)
                if t == NT - 1:
                    compose_w2(52, 56)
                if t + 1 < NT:
                    turn_probs(t + 1, 0)
                if t >= 1:
                    turn_attention(t - 1)
                if t == NT - 1:
                    compose_w2(56, 58)
                if t >= 3:
                    turn_ln2(t - 3)
                weigh_values(t, 1)
                if t >= 1:
                    project(t - 1)

            def ffn_hidden(b, j):
                pe.wait_ge(s_x2t, TPB * (b + 1))
                if b == 0:
                    pe.wait_ge(s_pt, 2 * NT)
                    pe.wait_ge(s_z, NT)
                    if j == 2:
                        pe.wait_ge(s_w2, 2)
                else:
                    pe.wait_ge(s_h, FT * (b - 1) + j + 1)
                mm(bank[j], w1[:, j * P:(j + 1) * P], x2T[:, b], start=True, stop=True).then_inc(s_hps, 1)

            def ffn_out(u):
                b, first = divmod(u * UT, TPB)
                if u == 0:
                    pe.wait_ge(s_pt, 2 * NT)
                elif u == 1:
                    pe.wait_ge(s_ots, NT)
                elif u == 2:
                    pe.wait_ge(s_r2, NT)
                elif u == 3:
                    pe.wait_ge(s_x2t, NT)
                else:
                    pe.wait_ge(s_r3, u - 3)
                pe.wait_ge(s_h, FT * (b + 1))
                for i in range(UT):
                    for j in range(FT):
                        last = mm(bank[4 + u % 4][:, i * P:(i + 1) * P],
                                  hT[:, b % 2, j, (first + i) * P:(first + i + 1) * P], w2[:, j],
                                  start=(j == 0), stop=(j == FT - 1))
                last.then_inc(s_fps, 1)

            ffn_hidden(0, 0)
            turn_back(NT - 1)
            compose_w2(58, FT * KT)
            turn_attention(NT - 1)
            turn_ln2(NT - 3)
            project(NT - 1)
            ffn_hidden(0, 1)
            turn_ln2(NT - 2)
            ffn_hidden(0, 2)
            ffn_hidden(0, 3)
            turn_ln2(NT - 1)
            for b in range(1, B + 1):
                if b < B:
                    for j in range(FT):
                        ffn_hidden(b, j)
                for u in range(NU // B * (b - 1), NU // B * b):
                    ffn_out(u)

        @block.scalar
        def _(act):
            def col(c):
                return vec[:, c:c + 1]

            fn = nc.scalar.activation
            act.wait_ge(s_abs, 1)
            fn(spt[:, 1:2], spt[:, 0:1], ACT.Exp, scale=-1.0).then_inc(s_sp_e, 1)
            act.wait_ge(s_lmax, 1)
            for i in range(2):
                last = fn(lg[:, i], lg[:, i], ACT.Exp, bias=lgm[:, i:i + 1], accum_out=lgs[:, i:i + 1])
            last.then_inc(s_lexp, 1)
            act.wait_ge(s_sp_e, 1)
            fn(spt[:, 2:3], spt[:, 1:2], ACT.Ln, bias=1.0).then_inc(s_sp_l, 1)
            act.wait_ge(s_const, 2)
            for b in range(B):
                act.wait_ge(s_x1ps, b + 1)
                fn(x1p[:, b, TW - 1:], bank[b % 2], ACT.Identity, bias=col(V_BX)).then_inc(s_x1, 1)
                act.wait_ge(s_x1, b + 1)
                fn(x2[:, b], x1p[:, b, 0:T], ACT.Identity, scale=col(V_CW), bias=col(V_CB)).then_inc(s_tap0, 1)
            for b in range(B):
                act.wait_ge(s_yps, b + 1)
                fn(yy[:, b], bank[Y_BANKS[b]], ACT.Gelu, bias=col(V_BY)).then_inc(s_y, 1)
            for b in range(B):
                act.wait_ge(s_gxps, b + 1)
                fn(gx[:, b], bank[b % 2], ACT.Sigmoid, bias=col(V_GIB)).then_inc(s_gx, 1)
                act.wait_ge(s_gaps, b + 1)
                fn(aa[:, b], bank[2 + b % 2], ACT.Sigmoid, bias=col(V_GAB)).then_inc(s_ga, 1)
            act.wait_ge(s_nsp, 1)

            def decay(b):
                act.wait_ge(s_u, b + 1)
                fn(aa[:, b], aa[:, b], ACT.Exp, scale=spt[:, 4:5]).then_inc(s_a, 1)

            for b in range(B):
                act.wait_ge(s_ga, b + 1)
                fn(uu[:, b], aa[:, b], ACT.Exp, scale=spt[:, 5:6]).then_inc(s_u, 1)
            decay(0)
            decay(1)
            for b in range(B):
                act.wait_ge(s_uc, b + 1)
                fn(uu[:, b], uu[:, b], ACT.Sqrt, scale=-1.0, bias=1.0).then_inc(s_mult, 1)
            decay(2)
            decay(3)

            def take_w1():
                act.wait_ge(s_w1ps, 1)
                nc.scalar.copy(w1[:], MB).then_inc(s_w1, 1)

            def take_w2():
                act.wait_ge(s_w2ps, 1)
                nc.scalar.copy(w2[:, 0:FT - 1].rearrange("p j d -> p (j d)"), FB[:, 0:(FT - 1) * D]).then_inc(s_w2, 1)

            def take_w2_last():
                act.wait_ge(s_w2ps, 2)
                nc.scalar.copy(w2[:, FT - 1], bank[2][:, 0:D]).then_inc(s_w2, 1)

            def ln1(b):
                act.wait_ge(s_rstd, b + 1)
                for i in range(TPB):
                    last = fn(x1n[:, b * TPB + i], bank[3 + b % 2][:, i * P:(i + 1) * P], ACT.Identity,
                              scale=rs[:, b % 2, i:i + 1], bias=nb[:, b % 2, i:i + 1])
                last.then_inc(s_x1n, 1)

            def take_ln1(b):
                act.wait_ge(s_x1tps, b + 1)
                nc.scalar.copy(x2[:, b], OB).then_inc(s_x1t, 1)

            def take_q0():
                for g in range(NG):
                    act.wait_ge(s_q0ps, g + 1)
                    fn(qs[:, 0, g], bank[Q0_BANKS[g]], ACT.Identity,
                       bias=col(V_BQS + g)).then_inc(s_q0h, 1)

            def take_q(b):
                act.wait_ge(s_qps, b)
                act.wait_ge(s_hy, b + 1)
                fn(qh[:, b], MB, ACT.Identity, bias=col(V_BQ)).then_inc(s_qh, 1)

            def cap(t):
                act.wait_ge(s_z, t + 1)
                z = zb[t % 2][:, HALF:2 * HALF]
                fn(z, z, ACT.Relu, scale=-1.0).then_inc(s_zn, 1)

            def probs(t, f):
                n = 2 * t + f
                act.wait_ge(s_zn if f else s_zc, t + 1)
                if n >= 2:
                    act.wait_ge(s_ptps, n - 1)
                fn(pb[:, f, 0:HALF], zb[t % 2][:, f * HALF:(f + 1) * HALF], ACT.Exp,
                   scale=-1.0 if f else 1.0).then_inc(s_p, 1)

            def take_probs(t, f):
                n = 2 * t + f
                act.wait_ge(s_ptps, n + 1)
                if n >= 2:
                    act.wait_ge(s_ot, n - 1)
                nc.scalar.copy(ptb[:, f], PT).then_inc(s_pt, 1)

            def take_attention(t):
                act.wait_ge(s_ontps, t + 1)
                if t >= 2:
                    act.wait_ge(s_x2tps, t - 1)
                nc.scalar.copy(onT[:, t % 2], TA).then_inc(s_ont, 1)

            def take_out(t):
                act.wait_ge(s_ot, 2 * (t + 1))
                if t >= 1:
                    act.wait_ge(s_o, t)
                nc.scalar.copy(oT, AT).then_inc(s_ots, 1)

            def take_ln2(t):
                act.wait_ge(s_x2tps, t + 1)
                nc.scalar.copy(x2T[:, t // TPB, (t % TPB) * P:(t % TPB + 1) * P], TX).then_inc(s_x2t, 1)

            def ln2(t):
                act.wait_ge(s_rstd, B + t + 1)
                fn(x2n[:, t], r2[:, t % 2], ACT.Identity, scale=rs[:, t % 2, 0:1],
                   bias=nb[:, t % 2, 0:1]).then_inc(s_x2n, 1)

            ln1(0)
            take_w1()
            take_ln1(0)
            ln1(1)
            take_q0()
            take_ln1(1)
            ln1(2)
            take_q(1)
            probs(0, 0)
            cap(0)
            take_ln1(2)
            ln1(3)
            take_q(2)
            take_ln1(3)
            probs(0, 1)
            take_probs(0, 0)
            take_q(3)
            cap(1)
            take_w2()
            probs(1, 0)
            for t in range(NT):
                take_probs(t, 1)
                if t >= 3:
                    ln2(t - 3)
                if t + 1 < NT:
                    probs(t + 1, 1)
                    take_probs(t + 1, 0)
                if t >= 1:
                    take_attention(t - 1)
                take_out(t)
                if t >= 3:
                    take_ln2(t - 3)
                if t + 2 < NT:
                    cap(t + 2)
                    probs(t + 2, 0)

            def hidden(b, j):
                act.wait_ge(s_hps, FT * b + j + 1)
                if b >= 2:
                    act.wait_ge(s_fps, NU // B * (b - 1))
                fn(hT[:, b % 2, j], bank[j], ACT.Gelu_apprx_tanh).then_inc(s_h, 1)

            ln2(NT - 3)
            hidden(0, 0)
            take_attention(NT - 1)
            take_ln2(NT - 3)
            take_w2_last()
            ln2(NT - 2)
            hidden(0, 1)
            take_ln2(NT - 2)
            ln2(NT - 1)
            take_ln2(NT - 1)
            hidden(0, 2)
            hidden(0, 3)
            for b in range(1, B):
                for j in range(FT):
                    hidden(b, j)

        @block.vector
        def _(dve):
            steps = [0]

            def step(ins):
                steps[0] += 1
                ins.then_inc(s_dve, 1)
                dve.wait_ge(s_dve, steps[0])

            v = nc.vector
            v.memset(mhalf[:], -0.5).then_inc(s_const, 1)
            dve.wait_ge(ld["vec"], 16)
            step(v.tensor_scalar(spt[:, 6:7], vec[:, V_AP:V_AP + 1], -1.0, None, ALU.mult))
            v.tensor_tensor(spt[:, 0:1], spt[:, 6:7], vec[:, V_AP:V_AP + 1], ALU.max).then_inc(s_abs, 1)
            dve.wait_ge(ld["lg"], 16)
            step(v.tensor_reduce(lgm[:], lg[:], AX_X, ALU.max))
            v.tensor_scalar(lgm[:], lgm[:], -1.0, None, ALU.mult).then_inc(s_lmax, 1)
            dve.wait_ge(s_lexp, 1)
            step(v.reciprocal(lgs[:], lgs[:]))
            hp = P // 2
            for i in range(2):
                for q in range(2):
                    last = v.tensor_scalar(wsel[q * hp:(q + 1) * hp, i],
                                           lg[q * hp:(q + 1) * hp, i].rearrange("p (k q) -> p q k", q=2)[:, q],
                                           lgs[q * hp:(q + 1) * hp, i:i + 1], None, ALU.mult)
            last.then_inc(s_wsel, 1)
            dve.wait_ge(s_sp_l, 1)
            step(v.scalar_tensor_tensor(spt[:, 3:4], vec[:, V_AP:V_AP + 1], 0.0, spt[:, 2:3], ALU.max, ALU.add))
            step(v.tensor_scalar(spt[:, 4:5], spt[:, 3:4], -C_GATE, None, ALU.mult))
            v.tensor_scalar(spt[:, 5:6], spt[:, 3:4], -2.0 * C_GATE, None, ALU.mult).then_inc(s_nsp, 1)

            for b in range(B):
                dve.wait_ge(s_tap0, b + 1)
                for i in range(1, TW):
                    ins = v.scalar_tensor_tensor(x2[:, b], x1p[:, b, i:i + T], vec[:, V_CW + i:V_CW + i + 1],
                                                 x2[:, b], ALU.mult, ALU.add)
                    if i < TW - 1:
                        step(ins)
                ins.then_inc(s_x2, 1)
            dve.wait_ge(s_kps, 1)

            def of_k(q):
                return ((KPS[q, :, 0:B * M], kst[q, 0:NG - 1]),
                        (KPS[q, 0:2, B * M:B * M + 2 * M],
                         kst[q, NG - 1].rearrange("p (i m) -> p i m", i=2)))

            for src, dst in of_k(slice(0, P)):
                ins = v.tensor_scalar(dst, src, SCALE, None, ALU.mult)
            ins.then_inc(s_kh, 1)
            dve.wait_ge(s_kh, 1)
            for i in (1, 3):
                for src, dst in of_k(slice(32 * i, 32 * i + 32)):
                    ins = v.scalar_tensor_tensor(dst, src, SCALE, dst.bitcast(F32), ALU.mult, ALU.subtract)
            ins.then_inc(s_kl, 1)

            def cap_u(b):
                dve.wait_ge(s_u, b + 1)
                v.tensor_scalar(uu[:, b], uu[:, b], 1.0, None, ALU.min).then_inc(s_uc, 1)

            dve.wait_ge(s_vps, 1)
            v.tensor_copy(vt[:], bank[5][0:M]).then_inc(s_vt, 1)
            for b in range(B):
                cap_u(b)

            def recur(b):
                dve.wait_ge(s_mult, b + 1)
                dve.wait_ge(s_gin, b + 1)
                step(v.tensor_tensor(gx[:, b, 1:], gx[:, b, 1:], uu[:, b, 1:], ALU.mult))
                dve.wait_ge(s_a, b + 1)
                step(v.tensor_tensor_scan(uu[:, b], aa[:, b], gx[:, b], 0.0, ALU.mult, ALU.add))
                dve.wait_ge(s_y, b + 1)
                v.tensor_tensor(yy[:, b], yy[:, b], uu[:, b], ALU.mult).then_inc(s_hy, 1)

            def stats(src, slot, n):
                for i in range(n):
                    ins = v.bn_stats(st[:, slot, i], src(i))
                step(ins)
                for i in range(n):
                    ins = v.bn_aggr(mv[:, slot, i], st[:, slot, i])
                ins.then_inc(s_var, 1)

            def ln1_stats(b):
                dve.wait_ge(s_r1ps, b + 1)
                if b >= 2:
                    dve.wait_ge(s_x1n, b - 1)
                stats(lambda i: bank[3 + b % 2][:, i * P:(i + 1) * P], b % 2, TPB)

            def q0_low():
                hi = slice(P // 2, P)
                for g in range(NG):
                    dve.wait_ge(s_q0h, g + 1)
                    v.scalar_tensor_tensor(qs[hi, 0, g], bank[Q0_BANKS[g]][hi], vec[hi, V_BQS + g:V_BQS + g + 1],
                                           qs[hi, 0, g].bitcast(F32), ALU.add, ALU.subtract).then_inc(s_q0l, 1)

            def q_low(b):
                dve.wait_ge(s_qh, b)
                v.scalar_tensor_tensor(ql[:, b], MB, vec[:, V_BQ:V_BQ + 1], qh[:, b].bitcast(F32), ALU.add,
                                       ALU.subtract).then_inc(s_ql, 1)

            def top_score(t):
                dve.wait_ge(s_sps, t + 1)
                v.tensor_reduce(mx[:], SC.rearrange("p (h m) -> p h m", m=M), AX_X, ALU.max).then_inc(s_top, 1)

            def clip_top(t):
                dve.wait_ge(s_top, t + 1)
                v.tensor_scalar(mc[:], mx[:], CLAMP, -CLAMP, ALU.min, ALU.max).then_inc(s_ctop, 1)

            def shift_scores(t):
                dve.wait_ge(s_ctop, t + 1)
                if t >= 2:
                    dve.wait_ge(s_p, 2 * (t - 1))
                v.scalar_tensor_tensor(zb[t % 2].rearrange("p (h m) -> p h m", m=M),
                                       SC.rearrange("p (h m) -> p h m", m=M), -CLAMP,
                                       mc[:].unsqueeze(2).to_broadcast([P, H, M]),
                                       ALU.max, ALU.subtract).then_inc(s_z, 1)

            def cap_scores(t):
                dve.wait_ge(s_z, t + 1)
                v.tensor_scalar(zb[t % 2][:, 0:HALF], zb[t % 2][:, 0:HALF], 0.0, None, ALU.min).then_inc(s_zc, 1)

            def of_attention(c0, c1):
                return AN.rearrange("p (h c) -> p h c", c=VC)[:, :, c0:c1]

            def invert_sums(t):
                dve.wait_ge(s_o, t + 1)
                v.reciprocal(rden[:, t % 2].unsqueeze(2), of_attention(HD, VC)).then_inc(s_rden, 1)

            def norm_heads(t):
                if t >= 2:
                    dve.wait_ge(s_ontps, t - 1)
                dve.wait_ge(s_rden, t + 1)
                v.tensor_tensor(on[:, t % 2].rearrange("p (h c) -> p h c", c=HD), of_attention(0, HD),
                                rden[:, t % 2].unsqueeze(2).to_broadcast([P, H, HD]), ALU.mult).then_inc(s_on, 1)

            def add_attention(t):
                dve.wait_ge(s_rps, t + 1)
                if t == 0:
                    dve.wait_ge(s_x1b, B)
                if t >= 2:
                    dve.wait_ge(s_x2n, t - 1)
                v.tensor_tensor(r2[:, t % 2], MB[:, 0:P], x1n[:, t], ALU.add).then_inc(s_r2, 1)

            def ln2_stats(t):
                dve.wait_ge(s_r2, t + 1)
                if t < 2:
                    dve.wait_ge(s_x1n, B)
                v.bn_stats(st[:, t % 2, 0], r2[:, t % 2]).then_inc(s_st2, 1)

            def ln2_mean(t):
                dve.wait_ge(s_st2, t + 1)
                if t >= 2:
                    dve.wait_ge(s_rstd, B + t - 1)
                v.bn_aggr(mv[:, t % 2, 0], st[:, t % 2, 0]).then_inc(s_var, 1)

            recur(0)
            recur(1)
            ln1_stats(0)
            recur(2)
            ln1_stats(1)
            recur(3)
            q0_low()
            ln1_stats(2)
            top_score(0)
            clip_top(0)
            ln1_stats(3)
            shift_scores(0)
            cap_scores(0)
            q_low(1)
            top_score(1)
            q_low(2)
            clip_top(1)
            shift_scores(1)
            cap_scores(1)
            q_low(3)
            for t in range(NT + 2):
                if t >= 2:
                    ln2_stats(t - 2)
                if t + 2 < NT:
                    top_score(t + 2)
                if 1 <= t <= NT:
                    invert_sums(t - 1)
                if t + 2 < NT:
                    clip_top(t + 2)
                if 1 <= t <= NT:
                    norm_heads(t - 1)
                if t >= 2:
                    ln2_mean(t - 2)
                if t + 2 < NT:
                    shift_scores(t + 2)
                    cap_scores(t + 2)
                if 1 <= t <= NT:
                    add_attention(t - 1)

            def add_ffn(u):
                dve.wait_ge(s_fps, u + 1)
                if u >= 2:
                    dve.wait_ge(s_out, u - 1)
                v.tensor_tensor(rr[:, u % 2].rearrange("p t d -> p (t d)"), bank[4 + u % 4][:, 0:UT * P],
                                x2n[:, u * UT:(u + 1) * UT].rearrange("p t d -> p (t d)"),
                                ALU.add).then_inc(s_r3, 1)

            def ln3_stats(u):
                dve.wait_ge(s_r3, u + 1)
                for i in range(UT):
                    ins = v.bn_stats(st3[:, u % 2, i], rr[:, u % 2, i])
                step(ins)
                for i in range(UT):
                    ins = v.bn_aggr(mv3[:, u % 2, i], st3[:, u % 2, i])
                ins.then_inc(s_var3, 1)

            def ln3(u):
                dve.wait_ge(s_rstd3, u + 1)
                if u >= OT_N:
                    dve.wait_ge(s_st[u % OT_N], 16 * (u // OT_N))
                for i in range(UT):
                    ins = v.tensor_scalar(ot[:, u % OT_N, i], rr[:, u % 2, i], mv3[:, u % 2, i, 0:1],
                                          rs3[:, u % 2, i:i + 1], ALU.subtract, ALU.mult)
                ins.then_inc(s_out, 1)

            for u in range(NU + 1):
                if u < NU:
                    add_ffn(u)
                    ln3_stats(u)
                if u >= 1:
                    ln3(u - 1)

        @block.gpsimd
        def _(pool):
            g = nc.gpsimd
            g.memset(x1p[:, :, 0:TW - 1], 0.0).then_inc(s_const, 1)
            pool.wait_ge(ld["vm"], 16)
            g.tensor_copy(vhat[:].rearrange("p b f i h c -> p (b f) (i h) c")[:, :, :, HD],
                          vm[:].rearrange("p i h -> p (i h)").unsqueeze(1).to_broadcast([P, 2 * B, RT * HH])
                          ).then_inc(s_ones, 1)
            pool.wait_ge(s_wsel, 1)
            pool.wait_ge(ld["a1"], 16)
            g.tensor_tensor(a1[:], a1[:], wsel[:, 0, :].unsqueeze(2).to_broadcast([P, KT, D]),
                            ALU.mult).then_inc(s_a1w, 1)
            pool.wait_ge(ld["b2"], 16)
            g.tensor_tensor(b2s[:], b2s[:], wsel[:, 1, :].unsqueeze(2).to_broadcast([P, KT, D]),
                            ALU.mult).then_inc(s_b2w, 1)

            def gate_input(b):
                pool.wait_ge(s_gx, b + 1)
                g.tensor_tensor(gx[:, b], gx[:, b], x2[:, b], ALU.mult).then_inc(s_gin, 1)

            def add_x(b):
                pool.wait_ge(s_hy, b + 1)
                g.tensor_tensor(xc[:, b], xc[:, b], yy[:, b], ALU.add).then_inc(s_r1, 1)

            def add_bo(b):
                pool.wait_ge(s_x1tps, b + 1)
                x = x1n[:, b * TPB:(b + 1) * TPB]
                g.tensor_tensor(x, x, bor[:].unsqueeze(1).to_broadcast([P, TPB, D]), ALU.add).then_inc(s_x1b, 1)

            def part_heads(b):
                if b == 0:
                    pool.wait_ge(s_kl, 1)
                    pool.wait_ge(ld["hm"], 16)
                for gr in range(NG):
                    last = g.tensor_tensor(ks[:, b, gr].rearrange("p (h m) -> p h m", m=M),
                                           kst[:, gr, b * M:(b + 1) * M].bitcast(F32).unsqueeze(1).to_broadcast([P, 4, M]),
                                           hm[:].unsqueeze(2).to_broadcast([P, 4, M]), ALU.mult)
                last.then_inc(s_ks, 1)

            def v_heads(b):
                pool.wait_ge(s_vr, 16 * len(VR_CUTS))
                for f in range(2):
                    last = g.tensor_tensor(
                        vhat[:, b, f, :, :, 0:HD],
                        vr.rearrange("p i (n h c) -> p n i h c", n=2 * B, h=HH)[:, 2 * b + f],
                        vm[:].unsqueeze(3).to_broadcast([P, RT, HH, HD]), ALU.mult)
                last.then_inc(s_vhat, 1)

            steps = [0]

            def step(ins):
                steps[0] += 1
                ins.then_inc(s_pool, 1)
                pool.wait_ge(s_pool, steps[0])

            def root(n, slot, width):
                pool.wait_ge(s_var, n + 1)
                step(g.tensor_scalar(ve[:, slot, 0:width], mv[:, slot, 0:width, 1], EPS, 1.0, ALU.add, ALU.mult))
                step(g.tensor_tensor(rs[:, slot, 0:width], ve[:, slot, 0:width], mhalf[:, 0:width], ALU.pow))
                step(g.tensor_tensor(ve[:, slot, 0:width], mv[:, slot, 0:width, 0], rs[:, slot, 0:width], ALU.mult))
                g.tensor_scalar(nb[:, slot, 0:width], ve[:, slot, 0:width], 0.0, -1.0, ALU.add,
                                ALU.mult).then_inc(s_rstd, 1)

            def root3(u):
                pool.wait_ge(s_var3, u + 1)
                step(g.tensor_scalar(ve3[:, u % 2], mv3[:, u % 2, :, 1], EPS, 1.0, ALU.add, ALU.mult))
                g.tensor_tensor(rs3[:, u % 2], ve3[:, u % 2], mhalf[:, 0:UT], ALU.pow).then_inc(s_rstd3, 1)

            def zero_padding():
                pool.wait_ge(s_w1ps, 1)
                g.memset(pb[:, :, HALF:PADW], 0.0).then_inc(s_pad, 1)

            pool.wait_ge(s_const, 2)
            pool.wait_ge(ld["bo"], 16)
            gate_input(0)
            part_heads(0)
            gate_input(1)
            gate_input(2)
            add_x(0)
            add_x(1)
            root(0, 0, TPB)
            add_x(2)
            gate_input(3)
            root(1, 1, TPB)
            part_heads(1)
            add_x(3)
            root(2, 0, TPB)
            root(3, 1, TPB)
            part_heads(2)
            zero_padding()
            add_bo(0)
            v_heads(0)
            v_heads(1)
            add_bo(1)
            part_heads(3)
            add_bo(2)
            v_heads(2)
            add_bo(3)
            v_heads(3)
            for t in range(NT):
                root(B + t, t % 2, 1)
            for u in range(NU):
                root3(u)


def kernel(x, ctx_768, L0_attn_w_x, L0_attn_b_x, L0_attn_w_y, L0_attn_b_y, L0_attn_conv_w, L0_attn_conv_b,
           L0_attn_gi_w, L0_attn_gi_b, L0_attn_ga_w, L0_attn_ga_b, L0_attn_a_param, L0_xattn_Wq, L0_xattn_bq,
           L0_xattn_Wk, L0_xattn_bk, L0_xattn_Wv, L0_xattn_bv, L0_xattn_Wo, L0_xattn_bo, L0_ffn_fc1_A,
           L0_ffn_fc1_B, L0_ffn_fc2_A, L0_ffn_fc2_B, L0_ffn_fc1_logits, L0_ffn_fc2_logits):
    import concourse.bacc as bacc
    from concourse.bass_utils import run_bass_kernel_spmd

    c = np.ascontiguousarray
    a = {}
    a["xT"] = c(np.transpose(x, (2, 0, 1)))
    a["vecs"] = c(np.stack([*L0_attn_conv_w, L0_attn_b_x, L0_attn_b_y, L0_attn_conv_b, L0_attn_gi_b,
                            L0_attn_ga_b, L0_attn_a_param, L0_xattn_bq,
                            *np.tile(L0_xattn_bq.reshape(NG, D // NG), (1, 4))], axis=1))
    a["wpack"] = c(np.stack([L0_attn_w_x, L0_attn_w_y, L0_attn_gi_w, L0_attn_ga_w, L0_xattn_Wq, L0_xattn_Wo,
                             *(np.tile(L0_xattn_Wq[:, i:i + 32], (1, 4)) for i in range(0, D, 32))], axis=1))
    ctxT = np.transpose(ctx_768, (2, 0, 1))
    ctxT = np.concatenate([ctxT.reshape(DC, B * M), np.ones((1, B * M), np.float32)], axis=0)
    wk = np.concatenate([L0_xattn_Wk, L0_xattn_bk[None]], axis=0)
    wkv = np.concatenate([*(np.tile(wk[:, i:i + 32], (1, 4)) for i in range(0, D, 32)),
                          np.concatenate([L0_xattn_Wv, L0_xattn_bv[None]], axis=0)], axis=1)
    a["kvpack"] = c(np.concatenate([ctxT, wkv], axis=1))
    a["logits"] = c(np.stack([L0_ffn_fc1_logits, L0_ffn_fc2_logits]))
    a["a1T"] = c(np.transpose(np.transpose(L0_ffn_fc1_A, (0, 2, 1)).reshape(KT, P, D), (1, 0, 2)))
    a["b1"] = c(np.transpose(L0_ffn_fc1_B.reshape(KT, P, F), (1, 0, 2)))
    a["a2T"] = c(np.transpose(np.transpose(L0_ffn_fc2_A, (0, 2, 1)).reshape(KT, P, F), (1, 0, 2)))
    a["b2"] = c(np.transpose(L0_ffn_fc2_B.reshape(KT, P, D), (1, 0, 2)))
    a["ident"] = np.eye(P, dtype=np.float32)
    a["hmask"] = c(np.tile(np.repeat(np.eye(4, dtype=np.float32), HD, axis=0), (4, 1)))
    row = np.arange(PADW)
    a["vmask"] = c(np.transpose((row[:, None] // M == np.arange(HH)[None]).astype(np.float32).reshape(RT, P, HH),
                                (1, 0, 2)))
    a["bo"] = c(L0_xattn_bo)
    nc = bacc.Bacc("TRN2", target_bir_lowering=False, num_devices=1)
    names = ["xT", "vecs", "wpack", "kvpack", "logits", "a1T", "b1", "a2T", "b2", "ident", "hmask", "vmask", "bo"]
    arrays = {f"in_{n}": a[n] for n in names}
    args = [nc.dram_tensor(f"in_{n}", a[n].shape, F32, kind="ExternalInput").ap() for n in names]
    out = nc.dram_tensor("out", (B, T, D), F32, kind="ExternalOutput").ap()
    build(nc, *args, out)
    r = run_bass_kernel_spmd(nc, [arrays], core_ids=[0])
    return r.results[0]["out"]
```
